# Optimizing a Trainium2 kernel written in Bass

```python
import numpy as np
import jax
import jax.numpy as jnp

def _softmax(x, axis=-1):
    return jax.nn.softmax(x, axis=axis)

def _gelu(x):
    return jax.nn.gelu(x, approximate=True)

def _silu(x):
    return jax.nn.silu(x)

def _sigmoid(x):
    return jax.nn.sigmoid(x)

def _layernorm(x, axis=-1, eps=1e-05):
    m = jnp.mean(x, axis=axis, keepdims=True)
    v = jnp.var(x, axis=axis, keepdims=True)
    return (x - m) / jnp.sqrt(v + eps)

def _scatter_add(tgt, idx, src, axis=0):
    return tgt.at[idx].add(src)

def _segment_sum(src, seg, n):
    return jax.ops.segment_sum(src, seg, n)
kernel_name = 'mk_prb_d1_jaxref_r4_5f4b47'

def setup_inputs(seed: int=0):
    np.random.seed(seed)
    _w = jnp.asarray

    def _L0_attn_setup():
        import jax, jax.numpy as jnp
        import numpy as np
        key = jax.random.key(seed)
        k1, k2, k3, k4, k5 = jax.random.split(key, 5)
        B, S, D = (4, 1024, 512)
        x = jax.random.normal(k1, (B, S, D), dtype=jnp.float32)
        W_in = jax.random.normal(k2, (D, D), dtype=jnp.float32) / np.sqrt(D)
        W_out = jax.random.normal(k3, (D, D), dtype=jnp.float32) / np.sqrt(D)
        decay = jax.random.normal(k4, (D,), dtype=jnp.float32) * 0.1
        bias = jax.random.normal(k5, (D,), dtype=jnp.float32) * 0.02
        return {'x': x, 'W_in': W_in, 'W_out': W_out, 'decay': decay, 'bias': bias}
    _L0_attn_in = _L0_attn_setup()

    def _L0_ffn_setup():
        import jax, jax.numpy as jnp
        import numpy as np
        TOP_K = 6
        CAP_FACTOR = 2

        def _moe_block(x2d, wg_router, w_gate, w_up, w_down, ws_gate, ws_up, ws_down):
            T, D = x2d.shape
            E = wg_router.shape[0]
            scores = jax.nn.softmax(x2d @ wg_router.T, axis=-1)
            topk_w, topk_idx = jax.lax.top_k(scores, TOP_K)
            topk_w = topk_w / (jnp.sum(topk_w, axis=-1, keepdims=True) + 1e-20)
            flat_idx = topk_idx.reshape(-1)
            oh = jax.nn.one_hot(flat_idx, E, dtype=jnp.int32)
            pos = jnp.cumsum(oh, axis=0) - 1
            pos_in_e = jnp.take_along_axis(pos, flat_idx[:, None], axis=1)[:, 0]
            C = CAP_FACTOR * (T * TOP_K // E)
            valid = pos_in_e < C
            safe_pos = jnp.where(valid, pos_in_e, 0)
            tok_id = jnp.repeat(jnp.arange(T), TOP_K)
            vmask = valid[:, None].astype(x2d.dtype)
            x_rep = x2d[tok_id] * vmask
            xe = jnp.zeros((E, C, D), x2d.dtype).at[flat_idx, safe_pos].add(x_rep)
            g = jnp.einsum('ecd,edf->ecf', xe, w_gate)
            u = jnp.einsum('ecd,edf->ecf', xe, w_up)
            ye = jnp.einsum('ecf,efd->ecd', jax.nn.silu(g) * u, w_down)
            y_tok = ye[flat_idx, safe_pos] * vmask
            y = jnp.sum(y_tok.reshape(T, TOP_K, D) * topk_w[..., None], axis=1)
            sh = jax.nn.silu(x2d @ ws_gate) * (x2d @ ws_up) @ ws_down
            return y + sh
        key = jax.random.key(seed)
        ks = jax.random.split(key, 9)
        B, S, D, F, E = (1, 512, 512, 352, 32)
        FS = F * 2
        s = 0.02
        return {'hidden_states': jax.random.normal(ks[0], (B, S, D), jnp.float32), 'wg_router': jax.random.normal(ks[1], (E, D), jnp.float32) * s, 'w_gate': jax.random.normal(ks[2], (E, D, F), jnp.float32) * s, 'w_up': jax.random.normal(ks[3], (E, D, F), jnp.float32) * s, 'w_down': jax.random.normal(ks[4], (E, F, D), jnp.float32) * s, 'ws_gate': jax.random.normal(ks[5], (D, FS), jnp.float32) * s, 'ws_up': jax.random.normal(ks[6], (D, FS), jnp.float32) * s, 'ws_down': jax.random.normal(ks[7], (FS, D), jnp.float32) * s}
    _L0_ffn_in = _L0_ffn_setup()
    _d = {'L0_attn_x': _L0_attn_in['x'], 'L0_attn_W_in': _L0_attn_in['W_in'], 'L0_attn_W_out': _L0_attn_in['W_out'], 'L0_attn_decay': _L0_attn_in['decay'], 'L0_attn_bias': _L0_attn_in['bias'], 'L0_ffn_wg_router': _L0_ffn_in['wg_router'], 'L0_ffn_w_gate': _L0_ffn_in['w_gate'], 'L0_ffn_w_up': _L0_ffn_in['w_up'], 'L0_ffn_w_down': _L0_ffn_in['w_down'], 'L0_ffn_ws_gate': _L0_ffn_in['ws_gate'], 'L0_ffn_ws_up': _L0_ffn_in['ws_up'], 'L0_ffn_ws_down': _L0_ffn_in['ws_down']}
    _x0 = _d['L0_attn_x']
    _d['L0_attn_x'] = jax.random.normal(jax.random.fold_in(jax.random.key(seed), 1), (4, 512, 512), dtype=_x0.dtype)
    del _x0
    return _d

def reference(L0_attn_x, L0_attn_W_in, L0_attn_W_out, L0_attn_decay, L0_attn_bias, L0_ffn_wg_router, L0_ffn_w_gate, L0_ffn_w_up, L0_ffn_w_down, L0_ffn_ws_gate, L0_ffn_ws_up, L0_ffn_ws_down):

    def _L0_attn_ref(x, W_in, W_out, decay, bias):
        import jax, jax.numpy as jnp
        import numpy as np
        d = jax.nn.sigmoid(decay)
        projected = jnp.einsum('bsd,ed->bse', x, W_in)

        def step(state, seg_t):
            state = d * state + (1.0 - d) * seg_t
            return (state, state)
        init = jnp.zeros((x.shape[0], x.shape[2]), dtype=x.dtype)
        _, states = jax.lax.scan(step, init, jnp.swapaxes(projected, 0, 1))
        stacked = jnp.swapaxes(states, 0, 1)
        return jnp.einsum('bsd,ed->bse', stacked, W_out) + bias[None, None, :]

    def _L0_ffn_ref(hidden_states, wg_router, w_gate, w_up, w_down, ws_gate, ws_up, ws_down):
        import jax, jax.numpy as jnp
        import numpy as np
        TOP_K = 6
        CAP_FACTOR = 2

        def _moe_block(x2d, wg_router, w_gate, w_up, w_down, ws_gate, ws_up, ws_down):
            T, D = x2d.shape
            E = wg_router.shape[0]
            scores = jax.nn.softmax(x2d @ wg_router.T, axis=-1)
            topk_w, topk_idx = jax.lax.top_k(scores, TOP_K)
            topk_w = topk_w / (jnp.sum(topk_w, axis=-1, keepdims=True) + 1e-20)
            flat_idx = topk_idx.reshape(-1)
            oh = jax.nn.one_hot(flat_idx, E, dtype=jnp.int32)
            pos = jnp.cumsum(oh, axis=0) - 1
            pos_in_e = jnp.take_along_axis(pos, flat_idx[:, None], axis=1)[:, 0]
            C = CAP_FACTOR * (T * TOP_K // E)
            valid = pos_in_e < C
            safe_pos = jnp.where(valid, pos_in_e, 0)
            tok_id = jnp.repeat(jnp.arange(T), TOP_K)
            vmask = valid[:, None].astype(x2d.dtype)
            x_rep = x2d[tok_id] * vmask
            xe = jnp.zeros((E, C, D), x2d.dtype).at[flat_idx, safe_pos].add(x_rep)
            g = jnp.einsum('ecd,edf->ecf', xe, w_gate)
            u = jnp.einsum('ecd,edf->ecf', xe, w_up)
            ye = jnp.einsum('ecf,efd->ecd', jax.nn.silu(g) * u, w_down)
            y_tok = ye[flat_idx, safe_pos] * vmask
            y = jnp.sum(y_tok.reshape(T, TOP_K, D) * topk_w[..., None], axis=1)
            sh = jax.nn.silu(x2d @ ws_gate) * (x2d @ ws_up) @ ws_down
            return y + sh
        B, S, D = hidden_states.shape
        x2d = hidden_states.reshape(-1, D)
        out = _moe_block(x2d, wg_router, w_gate, w_up, w_down, ws_gate, ws_up, ws_down)
        return out.reshape(B, S, D)
    x = L0_attn_x
    xn = _layernorm(x, axis=-1)
    x = x + _L0_attn_ref(xn, L0_attn_W_in, L0_attn_W_out, L0_attn_decay, L0_attn_bias) + _L0_ffn_ref(xn, L0_ffn_wg_router, L0_ffn_w_gate, L0_ffn_w_up, L0_ffn_w_down, L0_ffn_ws_gate, L0_ffn_ws_up, L0_ffn_ws_down)
    return x

_drawn_inputs = setup_inputs


def setup_inputs(seed=0):
    import zlib

    import numpy as np

    out = dict(_drawn_inputs(seed))
    spreads = {}
    factors = {'L0_attn_bias': 3.441,
     'L0_ffn_wg_router': 4.271,
     'L0_ffn_w_gate': 3.891,
     'L0_ffn_w_up': 3.814,
     'L0_ffn_w_down': 3.816,
     'L0_attn_decay': 3.987}
    for name, (base, spread) in spreads.items():
        noise = np.random.default_rng([zlib.crc32(name.encode()), seed]).standard_normal(out[name].shape)
        drawn = base * np.exp(spread * noise) if base else spread * noise
        out[name] = jnp.asarray(drawn.astype(out[name].dtype))
    for name, factor in factors.items():
        out[name] = (out[name] * factor).astype(out[name].dtype)
    return out
```

```python
from contextlib import ExitStack

import concourse.bass as bass
from concourse import mybir

F32 = mybir.dt.float32
F32R = mybir.dt.float32r
BF16 = mybir.dt.bfloat16
I32 = mybir.dt.int32
U32 = mybir.dt.uint32
ALU = mybir.AluOpType
ACT = mybir.ActivationFunctionType
AX = mybir.AxisListType.X

P = 128
B, S, D = 4, 512, 512
T = B * S
TILES = T // P
DC = D // P
E, F, TOPK = 32, 352, 6
CAP = 2 * (T * TOPK // E)
FS = 2 * F
FC = 3
FLAST = F - (FC - 1) * P
EPB = 3
SHARED = 2 * TILES
FIRST_X = SHARED + EPB * E
XMAX = 64
BLOCKS = FIRST_X + XMAX
ROWS = T + P
MAIN_SLOTS = E * EPB * P
TABLE = MAIN_SLOTS + XMAX * P
GU = DC * F
WW = 2 * GU + FC * D
PIECES = ((0, GU), (GU, 2 * GU), (2 * GU, WW))
N_MAIN = 2
N_X = N_MAIN + E


def build(nc, x, w_in, w_out, decay, bias, wg, w_gate, w_up, w_down, ws_gate, ws_up, ws_down, out,
          xn_rows, table):
    with ExitStack() as ctx:
        def sb(name, shape, dt=F32):
            return ctx.enter_context(nc.sbuf_tensor(name, shape, dt))

        def ps(name, shape):
            return ctx.enter_context(nc.psum_tensor(name, shape, F32))

        def sem(name):
            return ctx.enter_context(nc.semaphore(name))

        w_hi = sb("w_hi", [P, 2, WW], F32R)
        w_lo = sb("w_lo", [P, 2, WW], F32R)
        raw = sb("raw", [P, 2, WW])
        xnT = sb("xnT", [P, DC, T])
        xring = sb("xring", [P, 8, D])
        rows = sb("rows", [P, 8 * D])
        xT_hi = sb("xT_hi", [P, 2, DC, P], F32R)
        xT_lo = sb("xT_lo", [P, 2, DC, P], F32R)
        hT_hi = sb("hT_hi", [P, FC, P], F32R)
        hT_lo = sb("hT_lo", [P, FC, P], F32R)
        ident = sb("ident", [P, P])
        before = sb("before", [P, P], BF16)
        ones = sb("ones", [P, P], BF16)
        bias_b = sb("bias_b", [P, D])
        wg_nat = sb("wg_nat", [E, D])
        wgT = sb("wgT", [P, DC, E])
        dec = sb("dec", [P, 4, DC])
        epst = sb("epst", [P, 1])
        stats = sb("stats", [P, 4, 6])
        mv = sb("mv", [P, TILES, 2])
        std = sb("std", [P, TILES])
        rstd = sb("rstd", [P, TILES])
        nmr = sb("nmr", [P, TILES])
        ra = sb("ra", [P, TILES * E])
        rb = sb("rb", [P, TILES * E])
        rc = sb("rc", [P, TILES * E])
        zrow = rc[:]
        eq = sb("eq", [P, TOPK, E, TILES], BF16)
        r16 = sb("r16", [P, 6, TILES])
        top8 = sb("top8", [P, TILES, 8])
        idx8 = sb("idx8", [P, TILES, 8], U32)
        idxf = sb("idxf", [P, TILES, 8])
        iota_e = sb("iota_e", [P, E])
        tok_id = sb("tok_id", [P, TILES])
        reset = sb("reset", [P, E, TILES])
        trash = sb("trash", [P, 1])
        e384 = sb("e384", [P, E])
        blk128 = sb("blk128", [P, XMAX])
        r32 = sb("r32", [P, 6, E])
        slot_f = sb("slot_f", [P, TOPK, TILES])
        slot_i = sb("slot_i", [P, TOPK * TILES, 1], I32)
        pay = sb("pay", [P, TOPK * TILES, 2])
        eidf = sb("eidf", [P, XMAX])
        eid = sb("eid", [P, XMAX], I32)
        cnt = sb("cnt", [P, 4])
        cnt_i = sb("cnt_i", [P, 3], I32)
        tabrow = sb("tabrow", [P, 2, 2 * P])
        ids = sb("ids", [P, BLOCKS], I32)
        wts = sb("wts", [P, BLOCKS])
        gidx = sb("gidx", [P, 2], I32)
        sidx = sb("sidx", [P, 2], I32)
        swt = sb("swt", [P, 2])
        ridx = sb("ridx", [P, 2], I32)
        rpay = sb("rpay", [P, 2, 2])

        xe = [rows[:, i * D:(i + 1) * D] for i in range(2)]
        y_sb = [rows[:, (2 + i) * D:(3 + i) * D] for i in range(2)]
        sg = rows[:, 4 * D:4 * D + F]
        h_sb = rows[:, 5 * D:5 * D + F]
        half = DC * D
        xb = [w[:, 0, 0:half].rearrange("p (c t) -> p c t", c=DC) for w in (w_hi, w_lo)]
        w_inT = [w[:, 0, half:2 * half].rearrange("p (c e) -> p c e", c=DC) for w in (w_hi, w_lo)]
        st = [w[:, 1, 0:half].rearrange("p (c t) -> p c t", c=DC) for w in (w_hi, w_lo)]
        w_outT = [w[:, 1, half:2 * half].rearrange("p (c e) -> p c e", c=DC) for w in (w_hi, w_lo)]
        nat = [raw[:, 1, i * half:(i + 1) * half].rearrange("p (j d) -> p j d", j=DC) for i in range(2)]
        scan = raw[:, 1, 0:half].rearrange("p (m t) -> p m t", m=DC)
        q_sb = [raw[:, 1, half + i * S:half + (i + 1) * S] for i in range(2)]

        p_tx = ps("p_tx", [P, 512])
        p_th = ps("p_th", [P, 512])
        p_g = ps("p_g", [P, 512])
        p_u = ps("p_u", [P, 512])
        p_y = [ps(f"p_y{i}", [P, 512]) for i in range(2)]
        p_a = ps("p_a", [P, 512])
        p_b = ps("p_b", [P, 512])
        p_gu = [p_g, p_u]

        s_x = [sem(f"x_loaded{i}") for i in range(2)]
        s_wgl = sem("wg_loaded")
        s_decl = sem("decay_loaded")
        s_nat = [sem(f"nat_loaded{i}") for i in range(2)]
        s_biasl = sem("bias_loaded")
        s_ident = sem("ident_ready")
        s_const = sem("consts_ready")
        s_pool0 = sem("pool_setup_chain")
        s_zero = sem("zero_rows_stored")
        s_pre = sem("table_prefilled")
        s_rawz = sem("raw_tail_set")
        s_var = sem("variance_ready")
        s_std = sem("std_ready")
        s_norm = sem("norm_factors_ready")
        s_xn = sem("xn_ready")
        s_xns = [sem(f"xn_stored{i}") for i in range(2)]
        s_xnt = sem("xn_transposed")
        s_xnT = sem("xnT_ready")
        s_wgt = sem("wg_transposed")
        s_wgT = sem("wgT_ready")
        s_wt = sem("w_transposed")
        s_wth = sem("wT_hi_ready")
        s_wT = sem("wT_ready")
        s_dec = sem("decay_chain")
        s_dece = sem("decay_exp")
        s_lg = sem("logits_ready")
        s_ch = sem("dve_chain")
        s_lgm = sem("logits_less_max")
        s_ex = sem("logits_exp")
        s_eq = sem("choices_ready")
        s_cn = sem("counts_ready")
        s_route = sem("routing_ready")
        s_xbh = sem("xb_hi_ready")
        s_xb = sem("xb_ready")
        s_in = sem("in_projected")
        s_q = sem("q_ready")
        s_sc = sem("scanned")
        s_sth = sem("states_hi_ready")
        s_st = sem("states_ready")
        s_out = sem("out_projected")
        s_xres = sem("x_plus_bias_ready")
        s_base = sem("base_ready")
        s_bst = [sem(f"base_stored{i}") for i in range(2)]
        s_ld = [[sem(f"raw_loaded_{'gud'[j]}{i}") for i in range(2)] for j in range(3)]
        s_wh = sem("weights_hi_ready")
        s_w = sem("weights_split")
        s_gi = sem("gather_index_staged")
        s_gat = [sem(f"gathered{i}") for i in range(2)]
        s_stg = sem("scatter_index_staged")
        s_scat = sem("scattered")
        s_turn = sem("pool_turn")
        s_ri = sem("route_entry_staged")
        s_rd = [sem(f"route_entry_stored{i}") for i in range(2)]
        s_tabl = sem("table_loaded")
        s_tabt = sem("table_transposed")
        s_tab = sem("table_ready")
        s_tx = sem("x_transposed")
        s_xth = sem("xT_hi_ready")
        s_xt = sem("xT_ready")
        s_gd = sem("gate_done")
        s_ud = sem("up_done")
        s_sg = sem("silu_ready")
        s_h = sem("h_ready")
        s_th = sem("h_transposed")
        s_hth = sem("hT_hi_ready")
        s_ht = sem("hT_ready")
        s_dd = sem("down_done")
        s_y = sem("y_ready")

        def loaded(j, n_half):
            return (2 if j == 2 else 1) * 16 * (n_half + 1)

        block = ctx.enter_context(nc.Block())

        @block.sync
        def _(sp):
            def load_x(r, b):
                if r >= 2 and r < 4:
                    sp.wait_ge(s_xn, 4 * (r - 1))
                sp.dma_start(xring[:, 4 * (r % 2):4 * (r % 2) + 4, :],
                             x[512 * b:512 * b + 512, :].rearrange("(i p) d -> p i d", p=P)
                             ).then_inc(s_x[r % 2], 16)

            def load_set(par, wait, g_src, u_src, d_src):
                for j, src in ((0, g_src), (1, u_src)):
                    if wait is not None:
                        sp.wait_ge(s_w, wait + j + 1)
                    lo, hi = PIECES[j]
                    sp.dma_start(raw[:, par, lo:hi].rearrange("p (c f) -> p c f", c=DC), src
                                 ).then_inc(s_ld[j][par], 16)
                if wait is not None:
                    sp.wait_ge(s_w, wait + 3)
                lo, hi = PIECES[2]
                full = (FC - 1) * P
                sp.dma_start(raw[:, par, lo:hi - D].rearrange("p (c d) -> p c d", d=D),
                             d_src(0, full).rearrange("(c p) d -> p c d", p=P)).then_inc(s_ld[2][par], 16)
                sp.dma_start(raw[0:FLAST, par, hi - D:hi], d_src(full, F)).then_inc(s_ld[2][par], 16)

            def shared_set(s):
                load_set(s, None,
                         ws_gate.rearrange("(p c) f -> p c f", c=DC)[:, :, s * F:(s + 1) * F],
                         ws_up.rearrange("(p c) f -> p c f", c=DC)[:, :, s * F:(s + 1) * F],
                         lambda a, z: ws_down[s * F + a:s * F + z, :])

            def expert_set(par, wait, e):
                load_set(par, wait,
                         w_gate[e].rearrange("(p c) f -> p c f", c=DC),
                         w_up[e].rearrange("(p c) f -> p c f", c=DC),
                         lambda a, z: w_down[e][a:z, :])

            load_x(0, 0)
            load_x(1, 1)
            for b in range(B):
                if b >= 2:
                    load_x(b, b)
                sp.wait_ge(s_xn, 4 * (b + 1))
                sp.dma_start(xn_rows[512 * b:512 * b + 512, :].rearrange("(i p) d -> p i d", p=P),
                             rows[:, (b % 2) * 2048:(b % 2) * 2048 + 2048].rearrange("p (i d) -> p i d", i=4)
                             ).then_inc(s_xns[b % 2], 16)
            sp.wait_ge(s_rawz, 2)
            shared_set(0)
            sp.wait_ge(s_xn, 16)
            load_x(4, 0)
            load_x(5, 1)
            for b in range(B):
                for i in range(4):
                    t = 4 * b + i
                    sp.wait_ge(s_base, t + 1)
                    sp.dma_start(out[P * t:P * (t + 1), :], y_sb[t % 2]).then_inc(s_bst[t % 2], 16)
                if b < 2:
                    load_x(6 + b, 2 + b)
            sp.wait_ge(s_st, 16)
            shared_set(1)

            with sp.Fori(0, E // 2) as it:
                for par in range(2):
                    expert_set(par, 6 * it + 3 * par, 2 * it + par)
            sp.wait_ge(s_route, 1)
            pairs = sp.value_load(cnt_i[0:1, 0:1], min_val=2, max_val=XMAX // 2)
            with sp.Fori(0, pairs) as k:
                for par in range(2):
                    e = sp.value_load(eid[0:1, bass.ds(2 * k + par, 1)], min_val=0, max_val=E - 1)
                    expert_set(par, 6 * k + 3 * (E + par), e)

        @block.gpsimd
        def _(pool):
            g = nc.gpsimd
            g.memset(zrow, 0.0).then_inc(s_pool0, 1)
            g.memset(ident[:], 0.0).then_inc(s_pool0, 1)
            pool.wait_ge(s_pool0, 2)
            g.affine_select(out=ident[:], in_=ident[:], compare_op=ALU.not_equal, fill=1.0, base=0,
                            pattern=[[-1, P]], channel_multiplier=1).then_inc(s_ident, 1)
            g.memset(raw[:, 0, WW - D:WW], 0.0).then_inc(s_rawz, 1)
            g.memset(raw[:, 1, 2 * half:WW], 0.0).then_inc(s_rawz, 1)
            for dst in (xn_rows, out):
                pool.dma_start(dst[T:ROWS, :], zrow).then_inc(s_zero, 16)
            tr = tabrow[:, 0, :].rearrange("p (s two) -> p s two", two=2)
            g.memset(tabrow[:, 0, :], 0.0).then_inc(s_pool0, 1)
            pool.wait_ge(s_pool0, 3)
            g.iota(tr[:, :, 0], pattern=[[1, P]], base=T, channel_multiplier=0,
                   allow_small_or_imprecise_dtypes=True).then_inc(s_pool0, 1)
            pool.wait_ge(s_pool0, 4)
            tb = table[0:TABLE, :].rearrange("(b s) two -> b (s two)", s=P)
            pool.dma_start(tb[0:P, :], tabrow[:, 0, :]).then_inc(s_pre, 16)
            pool.dma_start(tb[P:TABLE // P, :], tabrow[0:TABLE // P - P, 0, :]).then_inc(s_pre, 16)

            def io(ap, pattern, base, mult):
                g.iota(ap, pattern=pattern, base=base, channel_multiplier=mult,
                       allow_small_or_imprecise_dtypes=True).then_inc(s_const, 1)

            io(iota_e[:], [[1, E]], 0, 0)
            io(tok_id[:], [[P, TILES]], 0, 1)
            io(ids[:, 0:SHARED].rearrange("p (a i) -> p a i", a=2), [[0, 2], [P, TILES]], 0, 1)
            io(trash[:], [[0, 1]], TABLE, 1)
            io(e384[:], [[EPB * P, E]], 0, 0)
            io(blk128[:], [[P, XMAX]], 0, 0)
            g.memset(wts[:, 0:SHARED], 1.0).then_inc(s_const, 1)
            g.memset(ones[:], 1.0).then_inc(s_const, 1)
            g.memset(before[:], 1.0).then_inc(s_const, 1)
            g.memset(reset[:], 1.0).then_inc(s_const, 1)
            pool.wait_ge(s_const, 10)
            g.affine_select(out=before[:], in_=before[:], compare_op=ALU.is_gt, fill=0.0, base=0,
                            pattern=[[1, P]], channel_multiplier=-1).then_inc(s_const, 1)
            g.memset(reset[:, :, 0:1], 0.0).then_inc(s_const, 1)

            pool.wait_ge(s_biasl, 16)
            for b in range(B):
                pool.wait_ge(s_x[b % 2], 16 * (b // 2 + 3))
                xr = xring[:, 4 * (b % 2):4 * (b % 2) + 4, :]
                g.tensor_tensor(xr, xr, bias_b[:].unsqueeze(1).to_broadcast([P, 4, D]), ALU.add
                                ).then_inc(s_xres, 1)

            def wait(semaphore, value):
                pool.wait_ge(semaphore, value)
                pool.sem_inc(s_turn, 1)

            def gather(b, par):
                g.tensor_copy(gidx[:, par:par + 1], ids[:, bass.ds(b, 1)]).then_inc(s_gi, 1)
                wait(s_gi, b + 1)
                pool.indirect_dma_start(
                    out=xe[par], out_offset=None, in_=xn_rows[:, :],
                    in_offset=bass.IndirectOffsetOnAxis(ap=gidx[:, par:par + 1], axis=0),
                    bounds_check=ROWS - 1).then_inc(s_gat[par], 16)

            def stage(b, par):
                g.tensor_copy(sidx[:, par:par + 1], ids[:, bass.ds(b, 1)]).then_inc(s_stg, 1)
                g.tensor_copy(swt[:, par:par + 1], wts[:, bass.ds(b, 1)]).then_inc(s_stg, 1)

            def scatter(par):
                pool.indirect_dma_start(
                    out=out[:, :], out_offset=bass.IndirectOffsetOnAxis(ap=sidx[:, par:par + 1], axis=0),
                    in_=y_sb[par], in_offset=None, bounds_check=ROWS - 1,
                    compute_op=ALU.add).then_inc(s_scat, 16)

            def route(c, par, left):
                if left is not None:
                    wait(s_rd[par], left)
                g.tensor_copy(ridx[:, par:par + 1], slot_i[:, bass.ds(c, 1), 0]).then_inc(s_ri, 1)
                g.tensor_copy(rpay[:, par, :], pay[:, bass.ds(c, 1), :].rearrange("p a b -> p (a b)")
                              ).then_inc(s_ri, 1)
                wait(s_ri, 2 * c + 2)
                pool.indirect_dma_start(
                    out=table[:, :], out_offset=bass.IndirectOffsetOnAxis(ap=ridx[:, par:par + 1], axis=0),
                    in_=rpay[:, par, :], in_offset=None,
                    bounds_check=TABLE + P - 1).then_inc(s_rd[par], 16)

            def step(b, par, first=None, last=None):
                if last is None:
                    wait(s_tx, b + 1)
                    gather(b + 2, par)
                if first is None:
                    wait(s_scat, 16 * (b - 1))
                if first != 0:
                    stage(b, par)
                    pool.wait_ge(s_y, b)
                    wait(s_stg, 2 * b)
                    scatter(1 - par)
                else:
                    stage(b, par)

            for i in range(2):
                pool.wait_ge(s_xns[i], 32)
            pool.wait_ge(s_zero, 32)
            pool.wait_ge(s_const, 12)
            pool.wait_ge(s_xnt, TILES)
            gather(0, 0)
            gather(1, 1)
            pool.wait_ge(s_route, 1)
            pool.wait_ge(s_pre, 32)
            for i in range(2):
                pool.wait_ge(s_bst[i], 16 * TILES // 2)
            R = 6
            for b in (0, 1):
                step(b, b, first=b)
                for c in range(R * b, R * b + R):
                    route(c, c % 2, None if c < 2 else 16 * (c // 2))
            with pool.Fori(0, 6) as it:
                for j in range(2):
                    step(2 * it + 2 + j, j)
                    for c in range(R * j, R * j + R):
                        route(12 * it + 12 + c, c % 2, 96 * it + 96 + 16 * (c // 2))
            for b in (14, 15):
                step(b, b % 2)
                for c in range(R * b, R * b + R):
                    route(c, c % 2, 16 * (c // 2))
            for b in (16, 17):
                step(b, b % 2)
            for i in range(2):
                pool.wait_ge(s_rd[i], 16 * TOPK * TILES // 2)
            pool.dma_start(tabrow[0:E * EPB, 0, :], tb[0:E * EPB, :]).then_inc(s_tabl, 16)
            pool.dma_start(tabrow[0:XMAX, 1, :], tb[E * EPB:TABLE // P, :]).then_inc(s_tabl, 16)
            with pool.Fori(0, 5) as it:
                for j in range(2):
                    step(2 * it + 18 + j, j)
            pool.wait_ge(s_tab, 4)
            for b in (28, 29, 30, 31):
                step(b, b % 2)
            with pool.Fori(0, E // 2) as it:
                for j in range(6):
                    step(6 * it + SHARED + j, j % 2)
            pairs = pool.value_load(cnt_i[0:1, 0:1], min_val=2, max_val=XMAX // 2)
            with pool.Fori(0, pairs - 1) as k:
                for j in range(2):
                    step(2 * k + FIRST_X + j, j)
            end = pool.snap(2 * pairs + FIRST_X)
            step(end - 2, 0, last=1)
            step(end - 1, 1, last=1)
            pool.wait_ge(s_scat, 16 * (end - 1))
            pool.wait_ge(s_y, end)
            wait(s_stg, 2 * end)
            scatter(1)
            pool.wait_ge(s_scat, 16 * end)

        @block.scalar
        def _(act):
            a = nc.scalar
            act.dma_start(wg_nat[:], wg).then_inc(s_wgl, 16)
            act.dma_start(dec[:, 0, :], decay.rearrange("(p m) -> p m", m=DC)).then_inc(s_decl, 16)
            act.wait_ge(s_rawz, 2)
            for i, w in ((0, w_in), (1, w_out)):
                act.dma_start(nat[i], w.rearrange("(j p) d -> p j d", p=P)).then_inc(s_nat[i], 16)
            act.dma_start(bias_b[:], bias.rearrange("(a n) -> a n", a=1).to_broadcast([P, D])
                          ).then_inc(s_biasl, 16)
            act.wait_ge(s_decl, 16)
            a.activation(dec[:, 1, :], dec[:, 0, :], ACT.Exp, scale=-1.0).then_inc(s_dece, 1)

            def copy(dst, src, scale=1.0):
                return a.activation(dst, src, ACT.Copy, scale=scale)

            def wT_hi(i, c):
                act.wait_ge(s_wt, 4 * i + c + 1)
                copy((w_inT, w_outT)[i][0][:, c, :], p_gu[c % 2][:]).then_inc(s_wth, 1)

            for b in range(B):
                act.wait_ge(s_var, b + 2)
                a.activation(std[:, 4 * b:4 * b + 4], mv[:, 4 * b:4 * b + 4, 1], ACT.Sqrt,
                             bias=epst[:]).then_inc(s_std, 1)
                act.wait_ge(s_norm, b + 1)
                if b >= 2:
                    act.wait_ge(s_xns[b % 2], 16)
                    act.wait_ge(s_xnt, 4 * (b - 1))
                for i in range(4):
                    t = 4 * b + i
                    a.activation(rows[:, (t % 8) * D:(t % 8 + 1) * D], xring[:, t % 8, :], ACT.Identity,
                                 scale=rstd[:, t:t + 1], bias=nmr[:, t:t + 1]).then_inc(s_xn, 1)
            for i in range(2):
                for c in range(DC):
                    wT_hi(i, c)

            def xb_hi(b):
                act.wait_ge(s_xnT, 4 * b + 4)
                if b >= 1:
                    act.wait_ge(s_in, 4 * b)
                copy(xb[0], xnT[:, :, b * S:(b + 1) * S]).then_inc(s_xbh, 1)

            def q(b):
                for m in range(DC):
                    act.wait_ge(s_in, 4 * b + m + 1)
                    if 4 * b + m >= 2:
                        act.wait_ge(s_sc, 4 * b + m - 1)
                    copy(q_sb[m % 2], p_gu[m % 2][:], scale=dec[:, 3, m:m + 1]).then_inc(s_q, 1)

            def st_hi(b):
                for m in range(DC):
                    act.wait_ge(s_sc, 4 * b + m + 1)
                    if b >= 1:
                        act.wait_ge(s_out, 4 * b)
                    copy(st[0][:, m, :], scan[:, m, :]).then_inc(s_sth, 1)

            def w_hi_piece(par, j, ld, free=None):
                act.wait_ge(s_ld[j][par], ld)
                if free is not None:
                    act.wait_ge(s_dd if j == 2 else s_ud, free)
                lo, hi = PIECES[j]
                copy(w_hi[:, par, lo:hi], raw[:, par, lo:hi]).then_inc(s_wh, 1)

            act.wait_ge(s_dec, 3)
            xb_hi(0)
            act.wait_ge(s_lgm, 1)
            a.activation(rb[:], ra[:], ACT.Exp).then_inc(s_ex, 1)
            for b in range(B):
                q(b)
                if b + 1 < B:
                    xb_hi(b + 1)
                st_hi(b)
            act.wait_ge(s_in, 16)
            for j in range(3):
                w_hi_piece(0, j, loaded(j, 0))

            def xt_hi(b, par):
                act.wait_ge(s_tx, b + 1)
                copy(xT_hi[:, par].rearrange("p c t -> p (c t)"), p_tx[:]).then_inc(s_xth, 1)

            def y_out(b, par):
                act.wait_ge(s_dd, b + 1)
                act.wait_ge(s_stg, 2 * b + 2)
                copy(y_sb[par], p_y[par][:], scale=swt[:, par:par + 1]).then_inc(s_y, 1)

            def step(b, par, pieces=(), first=None, last=None):
                act.wait_ge(s_gd, b + 1)
                a.activation(sg, p_g[:, 0:F], ACT.Silu).then_inc(s_sg, 1)
                if first != 0:
                    y_out(b - 1, 1 - par)
                act.wait_ge(s_th, b + 1)
                copy(hT_hi[:, 0:FC - 1].rearrange("p c t -> p (c t)"), p_th[:, 0:(FC - 1) * P])
                copy(hT_hi[0:FLAST, FC - 1], p_th[0:FLAST, (FC - 1) * P:FC * P]).then_inc(s_hth, 1)
                if last is None:
                    xt_hi(b + 2, par)
                for p in pieces:
                    w_hi_piece(*p)

            xt_hi(0, 0)
            xt_hi(1, 1)
            act.wait_ge(s_out, TILES)
            for i in range(2):
                act.wait_ge(s_bst[i], 16 * TILES // 2)
            step(0, 0, [(1, j, loaded(j, 0)) for j in (0, 1)], first=0)
            step(1, 1, [(1, 2, loaded(2, 0))])
            with act.Fori(0, 7) as it:
                for j in range(2):
                    step(2 * it + 2 + j, j)
            step(16, 0, [(0, 0, loaded(0, 1), 16)])
            step(17, 1, [(0, 1, loaded(1, 1), 16), (0, 2, loaded(2, 1), 16)])
            with act.Fori(0, 7) as it:
                for j in range(2):
                    step(2 * it + 18 + j, j)
            with act.Fori(0, E // 2) as it:
                for j in range(6):
                    ex, pc = divmod(j, EPB)
                    m = 2 if pc == 2 else 1
                    b0 = 6 * it + SHARED + EPB * ex
                    step(6 * it + SHARED + j, j % 2,
                         [(1 - ex, pc, m * 16 * (it + 2 + ex), b0)])
            for j in (0, 1):
                w_hi_piece(1, j, loaded(j, N_X // 2), FIRST_X)
            act.wait_ge(s_route, 1)
            pairs = act.value_load(cnt_i[0:1, 0:1], min_val=2, max_val=XMAX // 2)
            with act.Fori(0, pairs - 1) as k:
                for j in range(2):
                    b = 2 * k + FIRST_X + j
                    nh = k + N_X // 2
                    step(b, j, [(1 - j, 2, 32 * (nh + j + 1), b),
                                (j, 0, 16 * (nh + 2), b + 1),
                                (j, 1, 16 * (nh + 2), b + 1)])
            end = act.snap(2 * pairs + FIRST_X)
            nh = act.snap(pairs + N_X // 2)
            step(end - 2, 0, [(1, 2, 32 * nh, end - 2)], last=1)
            step(end - 1, 1, last=1)
            y_out(end - 1, 1)

        @block.tensor
        def _(pe):
            t_ = nc.tensor
            pe.wait_ge(s_ident, 1)
            pe.wait_ge(s_wgl, 16)
            for c in range(DC):
                last = t_.transpose(p_b[:, c * E:(c + 1) * E], wg_nat[:, c::DC], ident[0:E, 0:E])
            last.then_inc(s_wgt, 1)

            def tile_T(t):
                pe.wait_ge(s_xn, t + 1)
                if t >= 2:
                    pe.wait_ge(s_xnT, t - 1)
                for c in range(DC):
                    last = t_.transpose((p_tx, p_th)[t % 2][:, c * P:(c + 1) * P],
                                        rows[:, (t % 8) * D + c:(t % 8 + 1) * D:DC], ident[:])
                last.then_inc(s_xnt, 1)

            def logits(t):
                pe.wait_ge(s_xnT, t + 1)
                if t == 0:
                    pe.wait_ge(s_wgT, 1)
                for c in range(DC):
                    last = t_.matmul(p_a[:, t * E:(t + 1) * E], xnT[:, c, t * P:(t + 1) * P],
                                     wgT[:, c, :], start=(c == 0), stop=(c == DC - 1))
                last.then_inc(s_lg, 1)

            def w_T(i):
                pe.wait_ge(s_nat[i], 16)
                for c in range(DC):
                    n = 4 * i + c
                    if n >= 2:
                        pe.wait_ge(s_wT, n - 1)
                    for j in range(DC):
                        last = t_.transpose(p_gu[c % 2][:, j * P:(j + 1) * P], nat[i][:, j, c::DC],
                                            ident[:])
                    last.then_inc(s_wt, 1)

            for t in range(TILES):
                tile_T(t)
                if t >= 1:
                    logits(t - 1)
            logits(TILES - 1)
            w_T(0)
            w_T(1)

            def three(dst, stat, mov, first, last):
                t_.matmul(dst, stat[0], mov[0], start=first, stop=False)
                t_.matmul(dst, stat[0], mov[1], start=False, stop=False)
                return t_.matmul(dst, stat[1], mov[0], start=False, stop=last)

            def in_proj(b, first=False):
                pe.wait_ge(s_xb, b + 1)
                for m in range(DC):
                    if not first or m >= 2:
                        pe.wait_ge(s_q, 4 * b + m - 1)
                    for c in range(DC):
                        mm = three(p_gu[m % 2][:], [w[:, c, m::DC] for w in w_inT],
                                   [v[:, c, :] for v in xb], c == 0, c == DC - 1)
                    mm.then_inc(s_in, 1)

            def out_proj(b, first=False):
                pe.wait_ge(s_st, 4 * b + 4)
                for t in range(4):
                    if not first or t >= 2:
                        pe.wait_ge(s_base, 4 * b + t - 1)
                    for m in range(DC):
                        mm = three(p_y[t % 2][:], [v[:, m, t * P:(t + 1) * P] for v in st],
                                   [w[:, m, :] for w in w_outT], m == 0, m == DC - 1)
                    mm.then_inc(s_out, 1)

            def counts():
                pe.wait_ge(s_eq, 1)
                for dst, w in ((p_a, before), (p_b, ones)):
                    for k in range(TOPK):
                        last = t_.matmul(dst[:], w[:], eq[:, k].rearrange("p e i -> p (e i)"),
                                         start=(k == 0), stop=(k == TOPK - 1))
                last.then_inc(s_cn, 1)

            pe.wait_ge(s_wT, 8)
            in_proj(0, True)
            in_proj(1)
            out_proj(0, True)
            counts()
            with pe.Fori(0, 2) as b:
                in_proj(b + 2)
                out_proj(b + 1)

            def x_T(b, par, gathered, wait=True):
                pe.wait_ge(s_gat[par], gathered)
                if wait:
                    pe.wait_ge(s_xt, b)
                for c in range(DC):
                    last = t_.transpose(p_tx[:, c * P:(c + 1) * P], xe[par][:, c::DC], ident[:])
                last.then_inc(s_tx, 1)

            def up(b, par, wp, wneed):
                pe.wait_ge(s_xt, b + 1)
                for j, dst, done in ((0, p_g, s_gd), (1, p_u, s_ud)):
                    pe.wait_ge(s_w, wneed + 1 + j)
                    for c in range(DC):
                        lo = PIECES[j][0] + c * F
                        mm = three(dst[:, 0:F], [v[:, par, c, :] for v in (xT_hi, xT_lo)],
                                   [w[:, wp, lo:lo + F] for w in (w_hi, w_lo)], c == 0, c == DC - 1)
                    mm.then_inc(done, 1)

            def down(b, par, wp, wneed, wait=True):
                pe.wait_ge(s_ht, b + 1)
                pe.wait_ge(s_w, wneed + 3)
                if wait:
                    pe.wait_ge(s_y, b)
                for c in range(FC):
                    k = P if c < FC - 1 else FLAST
                    lo = PIECES[2][0] + c * D
                    mm = three(p_y[par][:], [v[0:k, c, :] for v in (hT_hi, hT_lo)],
                               [w[0:k, wp, lo:lo + D] for w in (w_hi, w_lo)], c == 0, c == FC - 1)
                mm.then_inc(s_dd, 1)

            def step(b, par, before_, after, gathered, first=None, last=None):
                if first != 0:
                    down(b - 1, 1 - par, *before_, wait=(first is None))
                pe.wait_ge(s_h, b + 1)
                for c in range(FC):
                    k = P if c < FC - 1 else FLAST
                    mm = t_.transpose(p_th[0:k, c * P:(c + 1) * P], h_sb[:, c * P:c * P + k], ident[:])
                mm.then_inc(s_th, 1)
                if last is None:
                    x_T(b + 2, par, gathered)
                if last != 2:
                    up(b + 1, 1 - par, *after)

            x_T(0, 0, 16, wait=False)
            x_T(1, 1, 16)
            out_proj(3)
            pe.wait_ge(s_q, 16)
            up(0, 0, 0, 0)
            pe.wait_ge(s_base, 16)
            step(0, 0, None, (0, 0), 32, first=0)
            step(1, 1, (0, 0), (0, 0), 32, first=1)
            with pe.Fori(0, 6) as it:
                for j in range(2):
                    step(2 * it + 2 + j, j, (0, 0), (0, 0), 16 * (it + 3))
            for b in (14, 15, 16, 17):
                step(b, b % 2, (0, 0) if b < 17 else (1, 3), (0, 0) if b < 15 else (1, 3),
                     16 * (b // 2 + 2))
            with pe.Fori(0, 5) as it:
                for j in range(2):
                    step(2 * it + 18 + j, j, (1, 3), (1, 3), 16 * (it + 11))
            pe.wait_ge(s_tabl, 32)
            n = E * EPB
            for w in range(2):
                t_.transpose(p_b[:, w * n:(w + 1) * n], tabrow[0:n, 0, w::2], ident[0:n, 0:n])
                last = t_.transpose(p_b[:, 2 * n + w * XMAX:2 * n + (w + 1) * XMAX],
                                    tabrow[0:XMAX, 1, w::2], ident[0:XMAX, 0:XMAX])
            last.then_inc(s_tabt, 1)
            for b in (28, 29, 30, 31):
                step(b, b % 2, (1, 3), (1, 3) if b < 31 else (0, 6), 16 * (b // 2 + 2))
            with pe.Fori(0, E // 2) as it:
                sets = ((1, 6 * it + 3), (0, 6 * it + 6), (1, 6 * it + 9), (0, 6 * it + 12))
                for j in range(2 * EPB):
                    step(6 * it + SHARED + j, j % 2, sets[(j - 1) // EPB + 1], sets[(j + 1) // EPB + 1],
                         16 * (3 * it + SHARED // 2 + j // 2 + 2))
            pe.wait_ge(s_route, 1)
            pairs = pe.value_load(cnt_i[0:1, 0:1], min_val=2, max_val=XMAX // 2)
            with pe.Fori(0, pairs - 1) as k:
                for j in range(2):
                    n3 = 6 * k + 3 * (N_X + j)
                    step(2 * k + FIRST_X + j, j, (1 - j, n3 - 3), (1 - j, n3 + 3),
                         16 * (k + FIRST_X // 2 + 2))
            end = pe.snap(2 * pairs + FIRST_X)
            n3 = pe.snap(6 * pairs + 3 * N_X)
            step(end - 2, 0, (1, n3 - 9), (1, n3 - 3), None, last=1)
            step(end - 1, 1, (0, n3 - 6), None, None, last=2)
            down(end - 1, 1, 1, n3 - 3)

        @block.vector
        def _(dve):
            v = nc.vector
            chain = [0]

            def link(ins):
                chain[0] += 1
                ins.then_inc(s_ch, 1)
                dve.wait_ge(s_ch, chain[0])

            def low(dst, src, hi):
                return v.tensor_tensor(dst, src, hi, ALU.subtract)

            v.memset(epst[:], 1e-5).then_inc(s_var, 1)
            dve.wait_ge(s_wgt, 1)
            v.tensor_copy(wgT[:].rearrange("p c e -> p (c e)"), p_b[:, 0:DC * E]).then_inc(s_wgT, 1)

            def tile_evac(t):
                dve.wait_ge(s_xnt, t + 1)
                v.tensor_copy(xnT[:, :, t * P:(t + 1) * P],
                              (p_tx, p_th)[t % 2][:].rearrange("p (c t) -> p c t", c=DC)
                              ).then_inc(s_xnT, 1)

            for b in range(B):
                dve.wait_ge(s_x[b % 2], 16 * (b // 2 + 1))
                bs = slice(4 * b, 4 * b + 4)
                for i in range(4):
                    ins = v.bn_stats(stats[:, i, :], xring[:, (4 * b + i) % 8, :])
                link(ins)
                for i in range(4):
                    ins = v.bn_aggr(mv[:, 4 * b + i, :], stats[:, i, :])
                ins.then_inc(s_var, 1)
                dve.wait_ge(s_std, b + 1)
                link(v.reciprocal(rstd[:, bs], std[:, bs]))
                v.scalar_tensor_tensor(out=nmr[:, bs], in0=mv[:, bs, 0], scalar=-1.0, in1=rstd[:, bs],
                                       op0=ALU.mult, op1=ALU.mult).then_inc(s_norm, 1)
                if b >= 1:
                    for t in range(4 * b - 4, 4 * b):
                        tile_evac(t)
            for t in range(TILES - 4, TILES):
                tile_evac(t)
            for i, w in enumerate((w_inT, w_outT)):
                for c in range(DC):
                    dve.wait_ge(s_wth, 4 * i + c + 1)
                    low(w[1][:, c, :], p_gu[c % 2][:], w[0][:, c, :]).then_inc(s_wT, 1)
            dve.wait_ge(s_dece, 1)
            v.tensor_scalar(dec[:, 2, :], dec[:, 1, :], 1.0, None, ALU.add).then_inc(s_dec, 1)
            dve.wait_ge(s_dec, 1)
            v.reciprocal(dec[:, 1, :], dec[:, 2, :]).then_inc(s_dec, 1)
            dve.wait_ge(s_dec, 2)
            v.tensor_scalar(dec[:, 3, :], dec[:, 1, :], -1.0, 1.0, ALU.mult, ALU.add).then_inc(s_dec, 1)

            def xb_lo(b):
                dve.wait_ge(s_xbh, b + 1)
                low(xb[1], xnT[:, :, b * S:(b + 1) * S], xb[0]).then_inc(s_xb, 1)

            def scans(b):
                for m in range(DC):
                    dve.wait_ge(s_q, 4 * b + m + 1)
                    if b >= 1:
                        dve.wait_ge(s_st, 4 * b)
                    v.tensor_tensor_scan(scan[:, m, :], dec[:, 1, m:m + 1].to_broadcast([P, S]),
                                         q_sb[m % 2], 0.0, ALU.mult, ALU.add).then_inc(s_sc, 1)

            def st_lo(b):
                for m in range(DC):
                    dve.wait_ge(s_sth, 4 * b + m + 1)
                    low(st[1][:, m, :], scan[:, m, :], st[0][:, m, :]).then_inc(s_st, 1)

            def base(b):
                dve.wait_ge(s_xres, b + 1)
                for t in range(4 * b, 4 * b + 4):
                    dve.wait_ge(s_out, t + 1)
                    if t >= 2:
                        dve.wait_ge(s_bst[t % 2], 16 * (t // 2))
                    v.tensor_tensor(y_sb[t % 2], p_y[t % 2][:], xring[:, 4 * (b % 2) + t % 4, :],
                                    ALU.add).then_inc(s_base, 1)

            xb_lo(0)

            def ie(ap):
                return ap.rearrange("p (i e) -> p i e", e=E)

            def ei(ap):
                return ap.rearrange("p (e i) -> p e i", e=E)

            def over_e(ap):
                return ap.unsqueeze(2).to_broadcast([P, TILES, E])

            def over_i(ap):
                return ap.unsqueeze(2).to_broadcast([P, E, TILES])

            dve.wait_ge(s_lg, TILES)
            link(v.tensor_reduce(r16[:, 0, :], ie(p_a[:]), AX, ALU.max))
            v.tensor_tensor(ie(ra[:]), ie(p_a[:]), over_e(r16[:, 0, :]), ALU.subtract).then_inc(s_lgm, 1)
            dve.wait_ge(s_ex, 1)
            link(v.tensor_reduce(r16[:, 1, :], ie(rb[:]), AX, ALU.add))
            link(v.reciprocal(r16[:, 2, :], r16[:, 1, :]))
            link(v.tensor_tensor(ie(ra[:]), ie(rb[:]), over_e(r16[:, 2, :]), ALU.mult))
            for i in range(TILES):
                ins = v.max(top8[:, i, :], ra[:, i * E:(i + 1) * E])
            link(ins)
            for i in range(TILES):
                ins = v.max_index(idx8[:, i, :], top8[:, i, :], ra[:, i * E:(i + 1) * E])
            link(ins)
            link(v.tensor_reduce(r16[:, 3, :], top8[:, :, 0:TOPK], AX, ALU.add))
            link(v.tensor_scalar(r16[:, 4, :], r16[:, 3, :], 1e-20, None, ALU.add))
            link(v.reciprocal(r16[:, 5, :], r16[:, 4, :]))
            link(v.tensor_copy(idxf[:], idx8[:]))
            dve.wait_ge(s_const, 12)
            for k in range(TOPK):
                ins = v.tensor_tensor(eq[:, k], over_i(iota_e[:]),
                                      idxf[:, :, k].unsqueeze(1).to_broadcast([P, E, TILES]), ALU.is_equal)
            ins.then_inc(s_eq, 1)
            by_ki = pay[:].rearrange("p (k i) two -> p k i two", k=TOPK)
            v.tensor_copy(by_ki[:, :, :, 0], tok_id[:].unsqueeze(1).to_broadcast([P, TOPK, TILES]))
            link(v.tensor_tensor(by_ki[:, :, :, 1], top8[:, :, 0:TOPK].rearrange("p i k -> p k i"),
                                 r16[:, 5, :].unsqueeze(1).to_broadcast([P, TOPK, TILES]), ALU.mult))

            def places():
                dve.wait_ge(s_cn, 1)
                dve.wait_ge(s_zero, 32)
                c_e, cap, nx, t1, xbase, shift = (r32[:, i, :] for i in range(6))
                rank = rc
                link(v.tensor_tensor_scan(rb[:], reset[:].rearrange("p e i -> p (e i)"), p_b[:], 0.0,
                                          ALU.mult, ALU.add))
                link(v.tensor_tensor(ra[:], rb[:], p_b[:], ALU.subtract))
                link(v.tensor_tensor(rank[:], ra[:], p_a[:], ALU.add))
                link(v.tensor_scalar(cap, ei(rb[:])[:, :, TILES - 1], float(CAP), -float(EPB * P),
                                     ALU.min, ALU.add))
                link(v.tensor_scalar(nx, cap, 0.0, float(P), ALU.is_gt, ALU.mult))
                for m in range(1, CAP // P - EPB):
                    link(v.tensor_scalar(t1, cap, float(m * P), float(P), ALU.is_gt, ALU.mult))
                    link(v.tensor_tensor(nx, nx, t1, ALU.add))
                xend = t1
                link(v.tensor_tensor_scan(xend, reset[:, :, 1], nx, 0.0, ALU.mult, ALU.add))
                link(v.tensor_tensor(xbase, xend, nx, ALU.subtract))
                link(v.scalar_tensor_tensor(out=shift, in0=xbase, scalar=float(MAIN_SLOTS - EPB * P),
                                            in1=e384[:], op0=ALU.add, op1=ALU.subtract))
                link(v.tensor_scalar(ra[:], rank[:], float(EPB * P), None, ALU.is_ge))
                link(v.tensor_tensor(ei(ra[:]), ei(ra[:]), over_i(shift), ALU.mult))
                link(v.tensor_tensor(ei(rb[:]), ei(rank[:]), over_i(e384[:]), ALU.add))
                link(v.tensor_tensor(rb[:], rb[:], ra[:], ALU.add))
                link(v.tensor_scalar(ra[:], rank[:], float(CAP), None, ALU.is_ge))
                link(v.scalar_tensor_tensor(out=rc[:], in0=rb[:], scalar=trash[:, 0:1], in1=ra[:],
                                            op0=ALU.subtract, op1=ALU.mult))
                link(v.tensor_tensor(rb[:], rb[:], rc[:], ALU.subtract))
                for k in range(TOPK):
                    link(v.tensor_tensor(ra[:], eq[:, k].rearrange("p e i -> p (e i)"), rb[:], ALU.mult))
                    link(v.tensor_reduce(slot_f[:, k, :], ra[:].rearrange("p (e i) -> p i e", e=E), AX,
                                         ALU.add))
                link(v.tensor_copy(slot_i[:].rearrange("p c one -> p (c one)"),
                                   slot_f[:].rearrange("p k i -> p (k i)")))
                w = TILES * E // E
                for k0 in range(0, XMAX, w):
                    link(v.tensor_tensor(ie(ra[:]), xend.unsqueeze(1).to_broadcast([P, w, E]),
                                         blk128[:, k0:k0 + w].unsqueeze(2).to_broadcast([P, w, E]),
                                         ALU.is_le))
                    link(v.tensor_reduce(eidf[:, k0:k0 + w], ie(ra[:]), AX, ALU.add))
                link(v.tensor_scalar(eid[:], eidf[:], float(E - 1), None, ALU.min))
                link(v.tensor_scalar(cnt_i[:, 1:2], xend[:, E - 1:E], float(2 * P - 1), None, ALU.add))
                link(v.tensor_scalar(cnt_i[:, 2:3], cnt_i[:, 1:2], 8, None, ALU.logical_shift_right))
                v.tensor_scalar(cnt_i[:, 0:1], cnt_i[:, 2:3], 2.0, None, ALU.max).then_inc(s_route, 1)

            for i in range(2):
                dve.wait_ge(s_xns[i], 32)
            for b in range(B):
                scans(b)
                if b + 1 < B:
                    xb_lo(b + 1)
                st_lo(b)
                if b == 1:
                    places()
                if b + 1 < B:
                    base(b)

            def w_lo_piece(par, j, nth):
                dve.wait_ge(s_wh, nth + 1)
                lo, hi = PIECES[j]
                low(w_lo[:, par, lo:hi], raw[:, par, lo:hi], w_hi[:, par, lo:hi]).then_inc(s_w, 1)

            def xt_lo(b, par):
                dve.wait_ge(s_xth, b + 1)
                low(xT_lo[:, par].rearrange("p c t -> p (c t)"), p_tx[:],
                    xT_hi[:, par].rearrange("p c t -> p (c t)")).then_inc(s_xt, 1)

            def step(b, par, pieces=(), last=None):
                dve.wait_ge(s_sg, b + 1)
                dve.wait_ge(s_ud, b + 1)
                v.tensor_tensor(h_sb, sg, p_u[:, 0:F], ALU.mult).then_inc(s_h, 1)
                dve.wait_ge(s_hth, b + 1)
                low(hT_lo[:, 0:FC - 1].rearrange("p c t -> p (c t)"), p_th[:, 0:(FC - 1) * P],
                    hT_hi[:, 0:FC - 1].rearrange("p c t -> p (c t)"))
                low(hT_lo[0:FLAST, FC - 1], p_th[0:FLAST, (FC - 1) * P:FC * P],
                    hT_hi[0:FLAST, FC - 1]).then_inc(s_ht, 1)
                if last is None:
                    xt_lo(b + 2, par)
                for p in pieces:
                    w_lo_piece(*p)

            for j in range(3):
                w_lo_piece(0, j, j)
            xt_lo(0, 0)
            xt_lo(1, 1)
            base(B - 1)
            step(0, 0, [(1, 0, 3), (1, 1, 4)])
            step(1, 1, [(1, 2, 5)])
            with dve.Fori(0, 7) as it:
                for j in range(2):
                    step(2 * it + 2 + j, j)
            step(16, 0, [(0, 0, 6)])
            step(17, 1, [(0, 1, 7), (0, 2, 8)])
            with dve.Fori(0, 5) as it:
                for j in range(2):
                    step(2 * it + 18 + j, j)
            dve.wait_ge(s_tabt, 1)
            n = E * EPB
            v.tensor_copy(ids[:, SHARED:FIRST_X], p_b[:, 0:n]).then_inc(s_tab, 1)
            v.tensor_copy(wts[:, SHARED:FIRST_X], p_b[:, n:2 * n]).then_inc(s_tab, 1)
            v.tensor_copy(ids[:, FIRST_X:BLOCKS], p_b[:, 2 * n:2 * n + XMAX]).then_inc(s_tab, 1)
            v.tensor_copy(wts[:, FIRST_X:BLOCKS], p_b[:, 2 * n + XMAX:2 * n + 2 * XMAX]).then_inc(s_tab, 1)
            for b in (28, 29, 30, 31):
                step(b, b % 2)
            with dve.Fori(0, E // 2) as it:
                for j in range(2 * EPB):
                    ex, pc = divmod(j, EPB)
                    step(6 * it + SHARED + j, j % 2, [(1 - ex, pc, 6 * it + 9 + j)])
            for j in (0, 1):
                w_lo_piece(1, j, 3 * (N_X + 1) + j)
            dve.wait_ge(s_route, 1)
            pairs = dve.value_load(cnt_i[0:1, 0:1], min_val=2, max_val=XMAX // 2)
            with dve.Fori(0, pairs - 1) as k:
                for j in range(2):
                    n3 = 6 * k + 3 * (N_X + j + 1)
                    step(2 * k + FIRST_X + j, j, [(1 - j, 2, n3 + 2), (j, 0, n3 + 3), (j, 1, n3 + 4)])
            end = dve.snap(2 * pairs + FIRST_X)
            n3 = dve.snap(6 * pairs + 3 * N_X)
            step(end - 2, 0, [(1, 2, n3 - 1)], last=1)
            step(end - 1, 1, last=1)


_INS = ("x", "W_in", "W_out", "decay", "bias")
_NAMES = ["L0_attn_" + n for n in _INS] + ["L0_ffn_" + n for n in
                                           ("wg_router", "w_gate", "w_up", "w_down", "ws_gate",
                                            "ws_up", "ws_down")]


def kernel(**inputs):
    import numpy as np
    import concourse.bacc as bacc
    from concourse.bass_utils import run_bass_kernel_spmd

    nc = bacc.Bacc("TRN2", target_bir_lowering=False, num_devices=1)
    arrays, args = {}, []
    for name in _NAMES:
        a = np.ascontiguousarray(inputs[name])
        if name == "L0_attn_x":
            a = a.reshape(T, D)
        arrays[name] = a
        args.append(nc.dram_tensor(name, a.shape, mybir.dt.from_np(a.dtype), kind="ExternalInput").ap())
    out = nc.dram_tensor("out", (ROWS, D), F32, kind="ExternalOutput").ap()
    xn_rows = nc.dram_tensor("xn_rows", (ROWS, D), F32, kind="Internal").ap()
    table = nc.dram_tensor("slot_table", (TABLE + P, 2), F32, kind="Internal").ap()
    build(nc, *args, out, xn_rows, table)
    r = run_bass_kernel_spmd(nc, [arrays], core_ids=[0])
    return r.results[0]["out"][0:T].reshape(B, S, D)
```

```python
from contextlib import ExitStack

import concourse.bass as bass
from concourse import mybir

F32 = mybir.dt.float32
F32R = mybir.dt.float32r
BF16 = mybir.dt.bfloat16
I32 = mybir.dt.int32
U32 = mybir.dt.uint32
ALU = mybir.AluOpType
ACT = mybir.ActivationFunctionType
AX = mybir.AxisListType.X

P = 128
B, S, D = 4, 512, 512
T = B * S
TILES = T // P
TPB = S // P
DC = D // P
E, F, TOPK = 32, 352, 6
CAP = 2 * (T * TOPK // E)
FC = 3
FLAST = F - (FC - 1) * P
SHARED = 2 * TILES
EPB = 3
MAINB = E * EPB
XMID = E // 2
XMAX = 64
COLS = MAINB + XMAX
ROWS = T + P
TABLE = COLS * P
GU = DC * F
WW = 2 * GU + FC * D
PIECES = ((0, GU), (GU, 2 * GU), (2 * GU, WW))

ROUNDS = E // 4
LEN = (EPB, EPB, 1, EPB, EPB, 1)
STEPS = sum(LEN)
MIDB = ROUNDS * STEPS
SET_OF = [m for m, n in enumerate(LEN) for _ in range(n)] + [6, 6]
LAST = [sum(LEN[:m + 1]) - 1 for m in range(6)]
SPLITS = [(1, 0), (1, 1), (1, 2), (2, 0), (2, 2), (3, 0), (3, 2),
          (4, 0), (4, 1), (4, 2), (5, 0), (5, 2), (6, 0), (6, 2)]
MIDDLE = {4: (2, 1), 6: (3, 1), 11: (5, 1), 13: (6, 1)}


def table_column(it, j):
    it, j = it + j // STEPS, j % STEPS
    if SET_OF[j] in (2, 5):
        return MAINB + 2 * it + SET_OF[j] // 3
    return 4 * EPB * it + j - SET_OF[j] // 3


def build(nc, x, w_in, w_out, decay, bias, wg, w_gate, w_up, w_down, ws_gate, ws_up, ws_down, out,
          xn_rows, table):
    with ExitStack() as ctx:
        def sb(name, shape, dt=F32):
            return ctx.enter_context(nc.sbuf_tensor(name, shape, dt))

        def ps(name, shape):
            return ctx.enter_context(nc.psum_tensor(name, shape, F32))

        def sem(name):
            return ctx.enter_context(nc.semaphore(name))

        w_hi = sb("w_hi", [P, 2, WW], F32R)
        w_lo = sb("w_lo", [P, 2, WW], F32R)
        raw = sb("raw", [P, 2, WW])
        xnT = sb("xnT", [P, DC, T])
        xring = sb("xring", [P, 4, D])
        rows = sb("rows", [P, 4 * D])
        sg = sb("sg", [P, F])
        h_sb = sb("h_sb", [P, F])
        xT_hi = sb("xT_hi", [P, 2, DC, P], F32R)
        xT_lo = sb("xT_lo", [P, 2, DC, P], F32R)
        hT_hi = sb("hT_hi", [P, FC, P], F32R)
        hT_lo = sb("hT_lo", [P, FC, P], F32R)
        inT_hi = sb("inT_hi", [P, DC, D], F32R)
        inT_lo = sb("inT_lo", [P, DC, D], F32R)
        ident = sb("ident", [P, P])
        before = sb("before", [P, P], BF16)
        ones = sb("ones", [P, P], BF16)
        bias_b = sb("bias_b", [P, D])
        wgT = sb("wgT", [P, DC, E])
        dec = sb("dec", [P, 4, DC])
        epst = sb("epst", [P, 1])
        stats = sb("stats", [P, 2, 6])
        mv = sb("mv", [P, TILES, 2])
        std = sb("std", [P, TILES])
        rstd = sb("rstd", [P, TILES])
        nmr = sb("nmr", [P, TILES])
        r16 = sb("r16", [P, 6, TILES])
        top8 = sb("top8", [P, TILES, 8])
        idx8 = sb("idx8", [P, TILES, 8], U32)
        idxf = sb("idxf", [P, TILES, 8])
        iota_e = sb("iota_e", [P, E])
        tok_id = sb("tok_id", [P, TILES])
        trash = sb("trash", [P, E])
        e384 = sb("e384", [P, E])
        blk128 = sb("blk128", [P, XMAX])
        r32 = sb("r32", [P, 7, E])
        slot_f = sb("slot_f", [P, TOPK, TILES])
        slot_i = sb("slot_i", [P, TOPK * TILES, 1], I32)
        pay = sb("pay", [P, TOPK * TILES, 2])
        eidf = sb("eidf", [P, XMAX])
        eid = sb("eid", [P, XMAX], I32)
        cnt_i = sb("cnt_i", [P, 4], I32)
        tabrow = sb("tabrow", [P, 2, 2 * P])
        ids = sb("ids", [P, COLS], I32)
        wts = sb("wts", [P, COLS])
        gidx = sb("gidx", [P, 2], I32)
        sidx = sb("sidx", [P, 2], I32)
        swt = sb("swt", [P, 2])
        ridx = sb("ridx", [P, 4], I32)
        rpay = sb("rpay", [P, 4, 2])

        xe = [rows[:, i * D:(i + 1) * D] for i in range(2)]
        y_sb = [rows[:, (2 + i) * D:(3 + i) * D] for i in range(2)]
        wg_nat = bias_b[0:E, :]
        half = DC * D
        xb = [w[:, 0, 0:half].rearrange("p (c t) -> p c t", c=DC) for w in (w_hi, w_lo)]
        w_inT = [inT_hi, inT_lo]
        st = [w[:, 1, 0:half].rearrange("p (c t) -> p c t", c=DC) for w in (w_hi, w_lo)]
        w_outT = [w[:, 1, half:2 * half].rearrange("p (c e) -> p c e", c=DC) for w in (w_hi, w_lo)]
        nat = [raw[:, 0, i * half:(i + 1) * half].rearrange("p (j d) -> p j d", j=DC) for i in range(2)]
        scan = raw[:, 1, 0:half].rearrange("p (m t) -> p m t", m=DC)
        q_sb = [raw[:, 1, half + i * S:half + (i + 1) * S] for i in range(2)]
        TE = TILES * E
        ra, rb, rc, reset = (raw[:, 1, i * TE:(i + 1) * TE] for i in range(4))
        eq = raw[:, 1, 4 * TE:4 * TE + TOPK * TE // 2].bitcast(BF16).rearrange(
            "p (k ei) -> p k ei", k=TOPK)

        p_tx = ps("p_tx", [P, 512])
        p_th = ps("p_th", [P, 512])
        p_g = ps("p_g", [P, 512])
        p_u = ps("p_u", [P, 512])
        p_y = [ps(f"p_y{i}", [P, 512]) for i in range(2)]
        p_a = ps("p_a", [P, 512])
        p_b = ps("p_b", [P, 512])
        p_gu = [p_g, p_u]

        s_x = [sem(f"x_loaded{i}") for i in range(4)]
        s_wgl = sem("wg_loaded")
        s_decl = sem("decay_loaded")
        s_nat = [sem(f"nat_loaded{i}") for i in range(2)]
        s_biasl = sem("bias_loaded")
        s_xbias = sem("x_plus_bias_ready")
        s_ident = sem("ident_ready")
        s_const = sem("consts_ready")
        s_pool0 = sem("pool_setup_chain")
        s_zero = sem("zero_rows_stored")
        s_pre = sem("table_prefilled")
        s_rawz = sem("raw_tail_set")
        s_eps = sem("eps_ready")
        s_var = sem("variance_ready")
        s_std = sem("std_ready")
        s_norm = sem("norm_factors_ready")
        s_xn = sem("xn_ready")
        s_xns = [sem(f"xn_stored{i}") for i in range(4)]
        s_xnt = sem("xn_transposed")
        s_xnT = sem("xnT_ready")
        s_wgt = sem("wg_transposed")
        s_wgT = sem("wgT_ready")
        s_wt = sem("w_transposed")
        s_wth = sem("wT_hi_ready")
        s_wT = sem("wT_ready")
        s_dec = sem("decay_chain")
        s_dece = sem("decay_exp")
        s_lg = sem("logits_ready")
        s_ch = sem("dve_chain")
        s_lgm = sem("logits_less_max")
        s_ex = sem("logits_exp")
        s_eq = sem("choices_ready")
        s_cn = sem("counts_ready")
        s_reset = sem("reset_ready")
        s_route = sem("routing_ready")
        s_xbh = sem("xb_hi_ready")
        s_xb = sem("xb_ready")
        s_in = sem("in_projected")
        s_q = sem("q_ready")
        s_sc = sem("scanned")
        s_sth = sem("states_hi_ready")
        s_st = sem("states_ready")
        s_out = sem("out_projected")
        s_base = sem("base_ready")
        s_bst = [sem(f"base_stored{i}") for i in range(2)]
        s_ysh = sem("shared_y_ready")
        s_sst = [sem(f"shared_y_stored{i}") for i in range(2)]
        s_ld = [[sem(f"raw_loaded_{'gud'[j]}{i}") for i in range(2)] for j in range(3)]
        s_wh = sem("weights_hi_ready")
        s_w = sem("weights_split")
        s_gi = sem("gather_index_staged")
        s_gat = [sem(f"gathered{i}") for i in range(2)]
        s_stg = sem("scatter_index_staged")
        s_scat = sem("scattered")
        s_turn = sem("pool_turn")
        s_ri = sem("route_entry_staged")
        s_rd = [sem(f"route_entry_stored{i}") for i in range(4)]
        s_tabl = sem("table_loaded")
        s_tabt = sem("table_transposed")
        s_tab = sem("table_ready")
        s_tx = sem("x_transposed")
        s_xth = sem("xT_hi_ready")
        s_xt = sem("xT_ready")
        s_gd = sem("gate_done")
        s_ud = sem("up_done")
        s_sg = sem("silu_ready")
        s_h = sem("h_ready")
        s_th = sem("h_transposed")
        s_hth = sem("hT_hi_ready")
        s_ht = sem("hT_ready")
        s_dd = sem("down_done")
        s_y = sem("y_ready")

        block = ctx.enter_context(nc.Block())

        def loaded(j, nth):
            return (2 if j == 2 else 1) * 16 * (nth + 1)

        @block.sync
        def _(sp):
            def load_tile(slot, src):
                sp.dma_start(xring[:, slot, :], src).then_inc(s_x[slot], 16)

            def tile_rows(dram, t):
                return dram[bass.ds(P * t, P), :]

            def load_set(par, wait, g_src, u_src, d_src):
                for j, src in ((0, g_src), (1, u_src)):
                    if wait is not None:
                        sp.wait_ge(s_w, wait + j + 1)
                    lo, hi = PIECES[j]
                    sp.dma_start(raw[:, par, lo:hi].rearrange("p (c f) -> p c f", c=DC), src
                                 ).then_inc(s_ld[j][par], 16)
                if wait is not None:
                    sp.wait_ge(s_w, wait + 3)
                lo, hi = PIECES[2]
                full = (FC - 1) * P
                sp.dma_start(raw[:, par, lo:hi - D].rearrange("p (c d) -> p c d", d=D),
                             d_src(0, full).rearrange("(c p) d -> p c d", p=P)).then_inc(s_ld[2][par], 16)
                sp.dma_start(raw[0:FLAST, par, hi - D:hi], d_src(full, F)).then_inc(s_ld[2][par], 16)

            def shared_set(s):
                load_set(s, None,
                         ws_gate.rearrange("(p c) f -> p c f", c=DC)[:, :, s * F:(s + 1) * F],
                         ws_up.rearrange("(p c) f -> p c f", c=DC)[:, :, s * F:(s + 1) * F],
                         lambda a, z: ws_down[s * F + a:s * F + z, :])

            def expert_set(par, wait, e):
                load_set(par, wait,
                         w_gate[e].rearrange("(p c) f -> p c f", c=DC),
                         w_up[e].rearrange("(p c) f -> p c f", c=DC),
                         lambda a, z: w_down[e][a:z, :])

            def extra_set(par, wait, k):
                e = sp.value_load(eid[0:1, bass.ds(k, 1)], min_val=0, max_val=E - 1)
                expert_set(par, wait, e)

            def store_xn(t):
                sp.wait_ge(s_xn, t + 1)
                sp.dma_start(tile_rows(xn_rows, t), rows[:, (t % 4) * D:(t % 4 + 1) * D]
                             ).then_inc(s_xns[t % 4], 16)

            for t in range(4):
                load_tile(t, tile_rows(x, t))
            sp.wait_ge(s_rawz, 1)
            shared_set(0)
            for t in range(4, TILES):
                sp.wait_ge(s_xn, t - 3)
                load_tile(t % 4, tile_rows(x, t))
                store_xn(t - 4)
                if t == 9:
                    sp.wait_ge(s_rawz, 2)
                    shared_set(1)
            for t in range(TILES - 4, TILES):
                store_xn(t)

            for t in range(4):
                load_tile(t, tile_rows(x, t))
            sp.wait_ge(s_w, 3)
            for i, w in ((0, w_in), (1, w_out)):
                sp.dma_start(nat[i], w.rearrange("(j p) d -> p j d", p=P)).then_inc(s_nat[i], 16)

            def store_shared(t, j):
                sp.wait_ge(s_ysh, t + 1)
                sp.dma_start(tile_rows(out, t), y_sb[j % 2]).then_inc(s_sst[j % 2], 16)

            with sp.Fori(0, 3) as it:
                for j in range(4):
                    store_shared(4 * it + j, j)
                    load_tile(j, tile_rows(x, 4 * it + 4 + j))
            for t in range(TILES - 4, TILES):
                store_shared(t, t % 4)

            for i in range(2):
                sp.wait_ge(s_sst[i], 16 * TILES // 2)
            for t in range(4):
                load_tile(t, tile_rows(out, t))

            def store_base(t, j):
                sp.wait_ge(s_base, t + 1)
                sp.dma_start(tile_rows(out, t), y_sb[j % 2]).then_inc(s_bst[j % 2], 16)

            sp.wait_ge(s_wt, 8)
            expert_set(0, None, 0)
            with sp.Fori(0, 3) as it:
                for j in range(4):
                    store_base(4 * it + j, j)
                    load_tile(j, tile_rows(out, 4 * it + 4 + j))
            sp.wait_ge(s_st, DC * B)
            expert_set(1, None, 1)
            for t in range(TILES - 4, TILES):
                store_base(t, t % 4)

            sp.wait_ge(s_route, 1)

            def round_sets(it, sets):
                for m in sets:
                    wait = 18 * it + 3 * m
                    if m in (2, 5):
                        extra_set(m % 2, wait, 2 * it + m // 3)
                    else:
                        expert_set(m % 2, wait, 4 * it + (0, 1, 0, 2, 3)[m])

            round_sets(0, range(2, 6))
            with sp.Fori(1, ROUNDS) as it:
                round_sets(it, range(6))
            more = sp.value_load(cnt_i[0:1, 0:1], min_val=0, max_val=(XMAX - XMID) // 2)
            with sp.If(more > 0):
                with sp.Fori(0, more) as k:
                    for par in range(2):
                        extra_set(par, 6 * k + 3 * (6 * ROUNDS + par), 2 * k + XMID + par)

        @block.gpsimd
        def _(pool):
            g = nc.gpsimd
            zrow = rows[:, 3 * D:4 * D]
            g.memset(ident[:], 0.0).then_inc(s_pool0, 1)
            pool.wait_ge(s_pool0, 1)
            g.affine_select(out=ident[:], in_=ident[:], compare_op=ALU.not_equal, fill=1.0, base=0,
                            pattern=[[-1, P]], channel_multiplier=1).then_inc(s_ident, 1)
            g.memset(zrow, 0.0).then_inc(s_pool0, 1)
            g.memset(raw[:, 0, WW - D:WW], 0.0).then_inc(s_rawz, 1)
            g.memset(raw[:, 1, WW - D:WW], 0.0).then_inc(s_rawz, 1)
            pool.wait_ge(s_pool0, 2)
            for dst in (xn_rows, out):
                pool.dma_start(dst[T:ROWS, :], zrow).then_inc(s_zero, 16)
            tr = tabrow[:, 0, :].rearrange("p (s two) -> p s two", two=2)
            g.memset(tabrow[:, 0, :], 0.0).then_inc(s_pool0, 1)
            pool.wait_ge(s_pool0, 3)
            g.iota(tr[:, :, 0], pattern=[[1, P]], base=T, channel_multiplier=0,
                   allow_small_or_imprecise_dtypes=True).then_inc(s_pool0, 1)
            pool.wait_ge(s_pool0, 4)
            tb = table[0:TABLE, :].rearrange("(b s) two -> b (s two)", s=P)
            pool.dma_start(tb[0:P, :], tabrow[:, 0, :]).then_inc(s_pre, 16)
            pool.dma_start(tb[P:COLS, :], tabrow[0:COLS - P, 0, :]).then_inc(s_pre, 16)

            def io(ap, pattern, base, mult):
                g.iota(ap, pattern=pattern, base=base, channel_multiplier=mult,
                       allow_small_or_imprecise_dtypes=True).then_inc(s_const, 1)

            io(iota_e[:], [[1, E]], 0, 0)
            io(tok_id[:], [[P, TILES]], 0, 1)
            io(trash[:], [[T, E]], TABLE, 0)
            io(e384[:], [[EPB * P, E]], 0, 0)
            io(blk128[:], [[P, XMAX]], 0, 0)
            g.memset(ones[:], 1.0).then_inc(s_const, 1)
            g.memset(before[:], 1.0).then_inc(s_const, 1)
            pool.wait_ge(s_const, 7)
            g.affine_select(out=before[:], in_=before[:], compare_op=ALU.is_gt, fill=0.0, base=0,
                            pattern=[[1, P]], channel_multiplier=-1).then_inc(s_const, 1)
            pool.wait_ge(s_w, 6)
            g.memset(reset, 1.0).then_inc(s_reset, 1)
            pool.wait_ge(s_reset, 1)
            g.memset(reset.rearrange("p (e i) -> p e i", i=TILES)[:, :, 0:1], 0.0).then_inc(s_reset, 1)

            def wait(semaphore, value):
                pool.wait_ge(semaphore, value)
                pool.sem_inc(s_turn, 1)

            def route(c, stage_, left):
                if left is not None:
                    wait(s_rd[stage_], left)
                g.tensor_copy(ridx[:, stage_:stage_ + 1], slot_i[:, bass.ds(c, 1), 0]).then_inc(s_ri, 1)
                g.tensor_copy(rpay[:, stage_, :], pay[:, bass.ds(c, 1), :].rearrange("p a b -> p (a b)")
                              ).then_inc(s_ri, 1)
                wait(s_ri, 2 * c + 2)
                pool.indirect_dma_start(
                    out=table[:, :], in_=rpay[:, stage_, :], in_offset=None,
                    out_offset=bass.IndirectOffsetOnAxis(ap=ridx[:, stage_:stage_ + 1], axis=0),
                    bounds_check=TABLE + T * E - 1).then_inc(s_rd[stage_], 16)

            entries = TOPK * TILES
            pool.wait_ge(s_route, 1)
            pool.wait_ge(s_pre, 32)
            for c in range(4):
                route(c, c, None)
            with pool.Fori(1, entries // 4) as it:
                for c in range(4):
                    route(4 * it + c, c, 16 * it)
            for i in range(4):
                pool.wait_ge(s_rd[i], 4 * entries)
            pool.dma_start(tabrow[0:MAINB, 0, :], tb[0:MAINB, :]).then_inc(s_tabl, 16)
            pool.dma_start(tabrow[0:XMAX, 1, :], tb[MAINB:COLS, :]).then_inc(s_tabl, 16)

            def gather(i, par, col):
                g.tensor_copy(gidx[:, par:par + 1], ids[:, bass.ds(col, 1)]).then_inc(s_gi, 1)
                wait(s_gi, i + 1)
                pool.indirect_dma_start(
                    out=xe[par], out_offset=None, in_=xn_rows[:, :],
                    in_offset=bass.IndirectOffsetOnAxis(ap=gidx[:, par:par + 1], axis=0),
                    bounds_check=ROWS - 1).then_inc(s_gat[par], 16)

            def stage(par, col):
                g.tensor_copy(sidx[:, par:par + 1], ids[:, bass.ds(col, 1)]).then_inc(s_stg, 1)
                g.tensor_copy(swt[:, par:par + 1], wts[:, bass.ds(col, 1)]).then_inc(s_stg, 1)

            def scatter(i, par):
                pool.wait_ge(s_y, i + 1)
                wait(s_stg, 2 * i + 2)
                pool.indirect_dma_start(
                    out=out[:, :], in_=y_sb[par], in_offset=None,
                    out_offset=bass.IndirectOffsetOnAxis(ap=sidx[:, par:par + 1], axis=0),
                    bounds_check=ROWS - 1, compute_op=ALU.add).then_inc(s_scat, 16)

            def step(i, par, col, col2):
                if col2 is not None:
                    wait(s_tx, i + 1)
                    gather(i + 2, par, col2)
                if not isinstance(i, int) or i >= 2:
                    wait(s_scat, 16 * (i - 1))
                stage(par, col)
                if not isinstance(i, int) or i >= 1:
                    scatter(i - 1, 1 - par)

            def columns(it, j):
                more_ = isinstance(it, int) and it == ROUNDS - 1 and j + 2 >= STEPS
                return table_column(it, j), None if more_ else table_column(it, j + 2)

            pool.wait_ge(s_tab, 4)
            pool.wait_ge(s_zero, 32)
            pool.wait_ge(s_sst[0], 16 * TILES // 2)
            for i in range(4):
                pool.wait_ge(s_xns[i], 16 * TILES // 4)
            gather(0, 0, 0)
            gather(1, 1, 1)
            for i in range(2):
                pool.wait_ge(s_bst[i], 16 * TILES // 2)
            for j in range(STEPS):
                step(j, j % 2, *columns(0, j))
            with pool.Fori(1, ROUNDS - 1) as it:
                for j in range(STEPS):
                    step(STEPS * it + j, j % 2, *columns(it, j))
            for j in range(STEPS):
                step(MIDB - STEPS + j, j % 2, *columns(ROUNDS - 1, j))
            wait(s_scat, 16 * (MIDB - 1))
            scatter(MIDB - 1, 1)
            pool.wait_ge(s_scat, 16 * MIDB)
            more = pool.value_load(cnt_i[0:1, 0:1], min_val=0, max_val=(XMAX - XMID) // 2)
            with pool.If(more > 0):
                with pool.Fori(0, more) as k:
                    i, col = 2 * k + MIDB, 2 * k + MAINB + XMID
                    for j in range(2):
                        wait(s_tx, i)
                        gather(i + j, j, col + j)
                    for j in range(2):
                        stage(j, col + j)
                    for j in range(2):
                        scatter(i + j, j)
                        wait(s_scat, 16 * (i + j + 1))

        @block.scalar
        def _(act):
            a = nc.scalar
            act.dma_start(wg_nat, wg).then_inc(s_wgl, 16)
            act.dma_start(dec[:, 0, :], decay.rearrange("(p m) -> p m", m=DC)).then_inc(s_decl, 16)
            act.wait_ge(s_decl, 16)
            a.activation(dec[:, 1, :], dec[:, 0, :], ACT.Exp, scale=-1.0).then_inc(s_dece, 1)

            def copy(dst, src, scale=1.0):
                return a.activation(dst, src, ACT.Copy, scale=scale)

            def w_hi_piece(par, j, ld, free=None):
                act.wait_ge(s_ld[j][par], ld)
                if free is not None:
                    act.wait_ge(s_dd if j == 2 else s_ud, free)
                lo, hi = PIECES[j]
                copy(w_hi[:, par, lo:hi], raw[:, par, lo:hi]).then_inc(s_wh, 1)

            act.wait_ge(s_eps, 1)
            for t in range(TILES):
                if t % 2 == 0:
                    act.wait_ge(s_var, t // 2 + 1)
                    a.activation(std[:, t:t + 2], mv[:, t:t + 2, 1], ACT.Sqrt, bias=epst[:]
                                 ).then_inc(s_std, 1)
                    act.wait_ge(s_norm, t // 2 + 1)
                if t >= 4:
                    act.wait_ge(s_xns[t % 4], 16 * (t // 4))
                    act.wait_ge(s_xnt, t - 3)
                elif t == 3:
                    act.wait_ge(s_zero, 32)
                a.activation(rows[:, (t % 4) * D:(t % 4 + 1) * D], xring[:, t % 4, :], ACT.Identity,
                             scale=rstd[:, t:t + 1], bias=nmr[:, t:t + 1]).then_inc(s_xn, 1)
                if t in (5, 8, 11):
                    w_hi_piece(0, t // 3 - 1, loaded(t // 3 - 1, 0))
            act.wait_ge(s_wgT, 1)
            act.dma_start(bias_b[:], bias.rearrange("(a n) -> a n", a=1).to_broadcast([P, D])
                          ).then_inc(s_biasl, 16)

            def x_hi(t, par):
                act.wait_ge(s_xnT, TILES)
                copy(xT_hi[:, par], xnT[:, :, bass.ds(P * t, P)]).then_inc(s_xth, 1)

            def silu_hT(b, y=None, piece=None):
                act.wait_ge(s_gd, b + 1)
                a.activation(sg[:], p_g[:, 0:F], ACT.Silu).then_inc(s_sg, 1)
                if piece is not None:
                    w_hi_piece(*piece)
                if y is not None:
                    y_out(*y)
                act.wait_ge(s_th, b + 1)
                copy(hT_hi[:, 0:FC - 1].rearrange("p c t -> p (c t)"), p_th[:, 0:(FC - 1) * P])
                copy(hT_hi[0:FLAST, FC - 1], p_th[0:FLAST, (FC - 1) * P:FC * P]).then_inc(s_hth, 1)

            def wT_hi(i, c):
                act.wait_ge(s_wt, 4 * i + c + 1)
                copy((w_inT, w_outT)[i][0][:, c, :], p_tx[:]).then_inc(s_wth, 1)

            def shared_pair(t, par, last=False, between=None):
                silu_hT(2 * t)
                if not last:
                    x_hi(t + 1, 1 - par)
                if between is not None:
                    wT_hi(*between[0])
                silu_hT(2 * t + 1)
                if between is not None:
                    wT_hi(*between[1])

            x_hi(0, 0)
            for j in range(3):
                w_hi_piece(1, j, loaded(j, 0))
            act.wait_ge(s_lgm, 1)
            a.activation(rb, ra, ACT.Exp).then_inc(s_ex, 1)
            for t in range(4):
                shared_pair(t, t % 2, between=None if t < 2 else [(0, 2 * t - 4), (0, 2 * t - 3)])
            with act.Fori(2, 7) as it:
                for j in range(2):
                    shared_pair(2 * it + j, j)
            shared_pair(14, 0)
            shared_pair(15, 1, last=True)

            def xb_hi(b):
                if b >= 1:
                    act.wait_ge(s_in, DC * b)
                copy(xb[0], xnT[:, :, b * S:(b + 1) * S]).then_inc(s_xbh, 1)

            def q(b):
                for m in range(DC):
                    act.wait_ge(s_in, DC * b + m + 1)
                    if DC * b + m >= 2:
                        act.wait_ge(s_sc, DC * b + m - 1)
                    copy(q_sb[m % 2], p_gu[m % 2][:], scale=dec[:, 3, m:m + 1]).then_inc(s_q, 1)
                    if b == 0:
                        wT_hi(1, m)

            def st_hi(b):
                for m in range(DC):
                    act.wait_ge(s_sc, DC * b + m + 1)
                    if b >= 1:
                        act.wait_ge(s_out, TPB * b)
                    copy(st[0][:, m, :], scan[:, m, :]).then_inc(s_sth, 1)

            xb_hi(0)
            act.wait_ge(s_dd, SHARED)
            act.wait_ge(s_dec, 3)
            for b in range(B):
                q(b)
                if b + 1 < B:
                    xb_hi(b + 1)
                st_hi(b)
            act.wait_ge(s_in, DC * B)
            for j in range(3):
                w_hi_piece(0, j, loaded(j, 1))

            def xt_hi(i, par):
                act.wait_ge(s_tx, i + 1)
                copy(xT_hi[:, par].rearrange("p c t -> p (c t)"), p_tx[:]).then_inc(s_xth, 1)

            def y_out(i, par):
                act.wait_ge(s_dd, i + SHARED + 1)
                act.wait_ge(s_stg, 2 * i + 2)
                copy(y_sb[par], p_y[par][:], scale=swt[:, par:par + 1]).then_inc(s_y, 1)

            def round_(it, first, last):
                def split(m, j):
                    nth = 3 * it + m // 2 + 1
                    free = STEPS * it + (LAST[m - 2] if m >= 2 else LAST[m - 2] - STEPS)
                    return m % 2, j, (2 if j == 2 else 1) * 16 * (nth + 1), free + SHARED + 1

                for j in range(STEPS):
                    i = STEPS * it + j
                    middle = j in MIDDLE and not (last and MIDDLE[j][0] == 6)
                    silu_hT(i + SHARED, None if first and j == 0 else (i - 1, 1 - j % 2),
                            split(*MIDDLE[j]) if middle else None)
                    if not last or j + 2 < STEPS:
                        xt_hi(i + 2, j % 2)
                    if not last or SPLITS[j][0] < 6:
                        w_hi_piece(*split(*SPLITS[j]))

            xt_hi(0, 0)
            xt_hi(1, 1)
            act.wait_ge(s_out, TILES)
            for i in range(2):
                act.wait_ge(s_bst[i], 16 * TILES // 2)
            act.wait_ge(s_route, 1)
            round_(0, True, False)
            with act.Fori(1, ROUNDS - 1) as it:
                round_(it, False, False)
            round_(ROUNDS - 1, False, True)
            y_out(MIDB - 1, 1)
            more = act.value_load(cnt_i[0:1, 0:1], min_val=0, max_val=(XMAX - XMID) // 2)
            with act.If(more > 0):
                with act.Fori(0, more) as k:
                    i = 2 * k + MIDB
                    for par in range(2):
                        for j in range(3):
                            w_hi_piece(par, j, (2 if j == 2 else 1) * 16 * (k + 3 * ROUNDS + 2),
                                       i + SHARED)
                    for j in range(2):
                        xt_hi(i + j, j)
                    silu_hT(i + SHARED)
                    silu_hT(i + SHARED + 1, (i, 0))
                    y_out(i + 1, 1)

        @block.tensor
        def _(pe):
            t_ = nc.tensor
            pe.wait_ge(s_ident, 1)
            pe.wait_ge(s_wgl, 16)
            for c in range(DC):
                last = t_.transpose(p_b[:, c * E:(c + 1) * E], wg_nat[:, c::DC], ident[0:E, 0:E])
            last.then_inc(s_wgt, 1)

            def tile_T(t):
                pe.wait_ge(s_xn, t + 1)
                if t >= 2:
                    pe.wait_ge(s_xnT, t - 1)
                for c in range(DC):
                    last = t_.transpose((p_tx, p_th)[t % 2][:, c * P:(c + 1) * P],
                                        rows[:, (t % 4) * D + c:(t % 4 + 1) * D:DC], ident[:])
                last.then_inc(s_xnt, 1)

            def logits(t):
                pe.wait_ge(s_xnT, t + 1)
                if t == 0:
                    pe.wait_ge(s_wgT, 1)
                for c in range(DC):
                    last = t_.matmul(p_a[:, t * E:(t + 1) * E], xnT[:, c, t * P:(t + 1) * P],
                                     wgT[:, c, :], start=(c == 0), stop=(c == DC - 1))
                last.then_inc(s_lg, 1)

            for t in range(TILES):
                tile_T(t)
                if t >= 1:
                    logits(t - 1)
            logits(TILES - 1)

            def w_T(i, c):
                n = DC * i + c
                pe.wait_ge(s_nat[i], 16)
                if n >= 1:
                    pe.wait_ge(s_wT, n)
                for j in range(DC):
                    last = t_.transpose(p_tx[:, j * P:(j + 1) * P], nat[i][:, j, c::DC], ident[:])
                last.then_inc(s_wt, 1)

            def three(dst, stat, mov, first, last):
                t_.matmul(dst, stat[0], mov[0], start=first, stop=False)
                t_.matmul(dst, stat[0], mov[1], start=False, stop=False)
                return t_.matmul(dst, stat[1], mov[0], start=False, stop=last)

            def up(x_ready, xpar, par, pieces):
                pe.wait_ge(s_xt, x_ready)
                for j, dst, done in ((0, p_g, s_gd), (1, p_u, s_ud)):
                    pe.wait_ge(s_w, pieces + 1 + j)
                    for c in range(DC):
                        lo = PIECES[j][0] + c * F
                        mm = three(dst[:, 0:F], [v[:, xpar, c, :] for v in (xT_hi, xT_lo)],
                                   [w[:, par, lo:lo + F] for w in (w_hi, w_lo)], c == 0, c == DC - 1)
                    mm.then_inc(done, 1)

            def down(b, bank, par, pieces, first=True, last=True):
                pe.wait_ge(s_ht, b + 1)
                pe.wait_ge(s_w, pieces + 3)
                for c in range(FC):
                    k = P if c < FC - 1 else FLAST
                    lo = PIECES[2][0] + c * D
                    mm = three(p_y[bank][:], [v[0:k, c, :] for v in (hT_hi, hT_lo)],
                               [w[0:k, par, lo:lo + D] for w in (w_hi, w_lo)],
                               first and c == 0, last and c == FC - 1)
                mm.then_inc(s_dd, 1)

            def h_T(b):
                pe.wait_ge(s_h, b + 1)
                for c in range(FC):
                    k = P if c < FC - 1 else FLAST
                    mm = t_.transpose(p_th[0:k, c * P:(c + 1) * P], h_sb[:, c * P:c * P + k], ident[:])
                mm.then_inc(s_th, 1)

            def counts():
                pe.wait_ge(s_eq, 1)
                for dst, w in ((p_a, before), (p_b, ones)):
                    for k in range(TOPK):
                        last = t_.matmul(dst[:], w[:], eq[:, k, :], start=(k == 0), stop=(k == TOPK - 1))
                last.then_inc(s_cn, 1)

            def shared_tile(t, par, first=False, last=False, between=None):
                if not first:
                    down(2 * t - 1, 1 - par, 1, 3, first=False)
                h_T(2 * t)
                if between is not None:
                    w_T(*between[0])
                up(t + 1, par, 1, 3)
                if not first and not (isinstance(t, int) and t == 1):
                    pe.wait_ge(s_ysh, t - 1)
                down(2 * t, par, 0, 0, last=False)
                h_T(2 * t + 1)
                if between is not None:
                    w_T(*between[1])
                if not last:
                    up(t + 2, 1 - par, 0, 0)

            up(1, 0, 0, 0)
            shared_tile(0, 0, first=True)
            shared_tile(1, 1)
            shared_tile(2, 0, between=((0, 0), (0, 1)))
            counts()
            shared_tile(3, 1, between=((0, 2), (0, 3)))
            with pe.Fori(2, 7) as it:
                for j in range(2):
                    shared_tile(2 * it + j, j)
            shared_tile(14, 0)
            shared_tile(15, 1, last=True)
            down(SHARED - 1, 1, 1, 3, first=False)

            def in_proj(b, first=False):
                pe.wait_ge(s_xb, b + 1)
                for m in range(DC):
                    if not first or m >= 2:
                        pe.wait_ge(s_q, DC * b + m - 1)
                    for c in range(DC):
                        mm = three(p_gu[m % 2][:], [w[:, c, m::DC] for w in w_inT],
                                   [v[:, c, :] for v in xb], c == 0, c == DC - 1)
                    mm.then_inc(s_in, 1)
                    if first:
                        w_T(1, m)

            def out_proj(b, first=False):
                pe.wait_ge(s_st, DC * b + DC)
                for t in range(TPB):
                    if not first or t >= 2:
                        pe.wait_ge(s_base, TPB * b + t - 1)
                    for m in range(DC):
                        mm = three(p_y[t % 2][:], [v[:, m, t * P:(t + 1) * P] for v in st],
                                   [w[:, m, :] for w in w_outT], m == 0, m == DC - 1)
                    mm.then_inc(s_out, 1)

            pe.wait_ge(s_wT, DC)
            in_proj(0, True)
            in_proj(1)
            pe.wait_ge(s_wT, 2 * DC)
            pe.wait_ge(s_ysh, TILES)
            out_proj(0, True)
            with pe.Fori(0, 2) as b:
                in_proj(b + 2)
                out_proj(b + 1)

            pe.wait_ge(s_tabl, 32)
            for w in range(2):
                t_.transpose(p_b[:, w * MAINB:(w + 1) * MAINB], tabrow[0:MAINB, 0, w::2],
                             ident[0:MAINB, 0:MAINB])
                last = t_.transpose(p_b[:, 2 * MAINB + w * XMAX:2 * MAINB + (w + 1) * XMAX],
                                    tabrow[0:XMAX, 1, w::2], ident[0:XMAX, 0:XMAX])
            last.then_inc(s_tabt, 1)

            def x_T(i, par, gathered):
                pe.wait_ge(s_gat[par], gathered)
                pe.wait_ge(s_xt, i + TILES)
                for c in range(DC):
                    last = t_.transpose(p_tx[:, c * P:(c + 1) * P], xe[par][:, c::DC], ident[:])
                last.then_inc(s_tx, 1)

            def round_(it, first, last):
                for j in range(STEPS):
                    i = STEPS * it + j
                    if not first or j >= 1:
                        m = SET_OF[j - 1] if j else -1
                        if not first or j >= 2:
                            pe.wait_ge(s_y, i - 1)
                        down(i + SHARED - 1, 1 - j % 2, m % 2, 18 * it + 3 * m + 6)
                    h_T(i + SHARED)
                    if not last or j + 2 < STEPS:
                        x_T(i + 2, j % 2, 16 * (STEPS // 2 * it + j // 2 + 2))
                    if not last or j + 1 < STEPS:
                        m = SET_OF[j + 1]
                        up(i + 2 + TILES, 1 - j % 2, m % 2, 18 * it + 3 * m + 6)

            out_proj(3)
            x_T(0, 0, 16)
            x_T(1, 1, 16)
            pe.wait_ge(s_q, DC * B)
            up(1 + TILES, 0, 0, 6)
            pe.wait_ge(s_base, TILES)
            round_(0, True, False)
            with pe.Fori(1, ROUNDS - 1) as it:
                round_(it, False, False)
            round_(ROUNDS - 1, False, True)
            pe.wait_ge(s_y, MIDB - 1)
            down(MIDB - 1 + SHARED, 1, 1, 18 * ROUNDS + 3)
            pe.wait_ge(s_route, 1)
            more = pe.value_load(cnt_i[0:1, 0:1], min_val=0, max_val=(XMAX - XMID) // 2)
            with pe.If(more > 0):
                with pe.Fori(0, more) as k:
                    i = 2 * k + MIDB
                    n3 = 6 * k + 18 * ROUNDS + 6
                    for j in range(2):
                        x_T(i + j, j, 16 * (k + MIDB // 2 + 1))
                    up(i + TILES + 1, 0, 0, n3)
                    h_T(i + SHARED)
                    up(i + TILES + 2, 1, 1, n3 + 3)
                    pe.wait_ge(s_y, i)
                    down(i + SHARED, 0, 0, n3)
                    h_T(i + SHARED + 1)
                    down(i + SHARED + 1, 1, 1, n3 + 3)

        @block.vector
        def _(dve):
            v = nc.vector
            chain = [0]

            def link(ins):
                chain[0] += 1
                ins.then_inc(s_ch, 1)
                dve.wait_ge(s_ch, chain[0])

            def low(dst, src, hi):
                return v.tensor_tensor(dst, src, hi, ALU.subtract)

            def w_lo_piece(par, j, nth):
                dve.wait_ge(s_wh, nth + 1)
                lo, hi = PIECES[j]
                low(w_lo[:, par, lo:hi], raw[:, par, lo:hi], w_hi[:, par, lo:hi]).then_inc(s_w, 1)

            v.memset(epst[:], 1e-5).then_inc(s_eps, 1)

            def tile_evac(t):
                dve.wait_ge(s_xnt, t + 1)
                v.tensor_copy(xnT[:, :, t * P:(t + 1) * P],
                              (p_tx, p_th)[t % 2][:].rearrange("p (c t) -> p c t", c=DC)
                              ).then_inc(s_xnT, 1)

            for t in range(0, TILES, 2):
                ts = slice(t, t + 2)
                for i in range(2):
                    dve.wait_ge(s_x[(t + i) % 4], 16 * (t // 4 + 1))
                    ins = v.bn_stats(stats[:, i, :], xring[:, (t + i) % 4, :])
                link(ins)
                for i in range(2):
                    ins = v.bn_aggr(mv[:, t + i, :], stats[:, i, :])
                ins.then_inc(s_var, 1)
                if t == 0:
                    dve.wait_ge(s_wgt, 1)
                    v.tensor_copy(wgT[:].rearrange("p c e -> p (c e)"), p_b[:, 0:DC * E]
                                  ).then_inc(s_wgT, 1)
                dve.wait_ge(s_std, t // 2 + 1)
                link(v.reciprocal(rstd[:, ts], std[:, ts]))
                v.scalar_tensor_tensor(out=nmr[:, ts], in0=mv[:, ts, 0], scalar=-1.0, in1=rstd[:, ts],
                                       op0=ALU.mult, op1=ALU.mult).then_inc(s_norm, 1)
                if t >= 2:
                    tile_evac(t - 2)
                    tile_evac(t - 1)
                if t in (8, 10, 12):
                    w_lo_piece(0, t // 2 - 4, t // 2 - 4)
            tile_evac(TILES - 2)
            tile_evac(TILES - 1)

            def decays():
                dve.wait_ge(s_dece, 1)
                v.tensor_scalar(dec[:, 2, :], dec[:, 1, :], 1.0, None, ALU.add).then_inc(s_dec, 1)
                dve.wait_ge(s_dec, 1)
                v.reciprocal(dec[:, 1, :], dec[:, 2, :]).then_inc(s_dec, 1)
                dve.wait_ge(s_dec, 2)
                v.tensor_scalar(dec[:, 3, :], dec[:, 1, :], -1.0, 1.0, ALU.mult, ALU.add
                                ).then_inc(s_dec, 1)

            def ie(ap):
                return ap.rearrange("p (i e) -> p i e", e=E)

            def ei(ap):
                return ap.rearrange("p (e i) -> p e i", i=TILES)

            def over_e(ap):
                return ap.unsqueeze(2).to_broadcast([P, TILES, E])

            def over_i(ap):
                return ap.unsqueeze(2).to_broadcast([P, E, TILES])

            def less_max():
                dve.wait_ge(s_lg, TILES)
                link(v.tensor_reduce(r16[:, 0, :], ie(p_a[:]), AX, ALU.max))
                v.tensor_tensor(ie(ra), ie(p_a[:]), over_e(r16[:, 0, :]), ALU.subtract
                                ).then_inc(s_lgm, 1)

            def softmax_top():
                dve.wait_ge(s_ex, 1)
                link(v.tensor_reduce(r16[:, 1, :], ie(rb), AX, ALU.add))
                link(v.reciprocal(r16[:, 2, :], r16[:, 1, :]))
                link(v.tensor_tensor(ie(ra), ie(rb), over_e(r16[:, 2, :]), ALU.mult))
                for i in range(TILES):
                    ins = v.max(top8[:, i, :], ra[:, i * E:(i + 1) * E])
                link(ins)

            def top_index():
                for i in range(TILES):
                    ins = v.max_index(idx8[:, i, :], top8[:, i, :], ra[:, i * E:(i + 1) * E])
                link(ins)
                link(v.tensor_copy(idxf[:], idx8[:]))

            def choices():
                dve.wait_ge(s_const, 8)
                for k in range(TOPK):
                    ins = v.tensor_tensor(ei(eq[:, k, :]), over_i(iota_e[:]),
                                          idxf[:, :, k].unsqueeze(1).to_broadcast([P, E, TILES]),
                                          ALU.is_equal)
                ins.then_inc(s_eq, 1)

            def payload():
                link(v.tensor_reduce(r16[:, 3, :], top8[:, :, 0:TOPK], AX, ALU.add))
                link(v.tensor_scalar(r16[:, 4, :], r16[:, 3, :], 1e-20, None, ALU.add))
                link(v.reciprocal(r16[:, 5, :], r16[:, 4, :]))
                by_ki = pay[:].rearrange("p (k i) two -> p k i two", k=TOPK)
                v.tensor_copy(by_ki[:, :, :, 0], tok_id[:].unsqueeze(1).to_broadcast([P, TOPK, TILES]))
                link(v.tensor_tensor(by_ki[:, :, :, 1], top8[:, :, 0:TOPK].rearrange("p i k -> p k i"),
                                     r16[:, 5, :].unsqueeze(1).to_broadcast([P, TOPK, TILES]), ALU.mult))

            cap, nx, xend, xbase, s0, shift, shift2 = (r32[:, i, :] for i in range(7))

            def ranks():
                dve.wait_ge(s_cn, 1)
                dve.wait_ge(s_reset, 2)
                link(v.tensor_tensor_scan(rb, reset, p_b[:], 0.0, ALU.mult, ALU.add))
                link(v.tensor_tensor(ra, rb, p_b[:], ALU.subtract))
                link(v.tensor_tensor(rc, ra, p_a[:], ALU.add))

            def extra_slots():
                link(v.tensor_scalar(cap, ei(rb)[:, :, TILES - 1], float(CAP), -float(EPB * P),
                                     ALU.min, ALU.add))
                link(v.tensor_scalar(nx, cap, 0.0, float(P), ALU.is_gt, ALU.mult))
                for m in range(1, CAP // P - EPB):
                    link(v.tensor_scalar(xend, cap, float(m * P), float(P), ALU.is_gt, ALU.mult))
                    link(v.tensor_tensor(nx, nx, xend, ALU.add))
                link(v.tensor_tensor_scan(xend, ei(reset)[:, :, 1], nx, 0.0, ALU.mult, ALU.add))
                link(v.tensor_tensor(xbase, xend, nx, ALU.subtract))

            def slots():
                link(v.tensor_scalar(s0, xbase, float(MAINB * P - EPB * P), None, ALU.add))
                link(v.tensor_tensor(shift, s0, e384[:], ALU.subtract))
                link(v.tensor_tensor(shift2, trash[:], s0, ALU.subtract))
                link(v.tensor_tensor(ei(rb), ei(rc), over_i(e384[:]), ALU.add))
                for least, by in ((EPB * P, shift), (CAP, shift2)):
                    link(v.tensor_scalar(ra, rc, float(least), None, ALU.is_ge))
                    link(v.tensor_tensor(ei(ra), ei(ra), over_i(by), ALU.mult))
                    link(v.tensor_tensor(rb, rb, ra, ALU.add))

            def choice_slots(ks):
                for k in ks:
                    link(v.tensor_tensor(ra, eq[:, k, :], rb, ALU.mult))
                    link(v.tensor_reduce(slot_f[:, k, :], ra.rearrange("p (e i) -> p i e", e=E), AX,
                                         ALU.add))

            def extra_experts():
                w = TE // E
                for k0 in range(0, XMAX, w):
                    link(v.tensor_tensor(ie(ra), xend.unsqueeze(1).to_broadcast([P, w, E]),
                                         blk128[:, k0:k0 + w].unsqueeze(2).to_broadcast([P, w, E]),
                                         ALU.is_le))
                    link(v.tensor_reduce(eidf[:, k0:k0 + w], ie(ra), AX, ALU.add))
                link(v.tensor_scalar(eid[:], eidf[:], float(E - 1), None, ALU.min))

            def routed():
                link(v.tensor_copy(slot_i[:].rearrange("p c one -> p (c one)"),
                                   slot_f[:].rearrange("p k i -> p (k i)")))
                link(v.tensor_scalar(cnt_i[:, 1:2], xend[:, E - 1:E], float(2 * P - 1), None, ALU.add))
                link(v.tensor_scalar(cnt_i[:, 2:3], cnt_i[:, 1:2], 8, None, ALU.logical_shift_right))
                v.tensor_scalar(cnt_i[:, 0:1], cnt_i[:, 2:3], -float(XMID // 2), 0.0, ALU.add, ALU.max
                                ).then_inc(s_route, 1)

            def h_hT(b, piece=None):
                dve.wait_ge(s_sg, b + 1)
                dve.wait_ge(s_ud, b + 1)
                v.tensor_tensor(h_sb[:], sg[:], p_u[:, 0:F], ALU.mult).then_inc(s_h, 1)
                if piece is not None:
                    w_lo_piece(*piece)
                dve.wait_ge(s_hth, b + 1)
                low(hT_lo[:, 0:FC - 1].rearrange("p c t -> p (c t)"), p_th[:, 0:(FC - 1) * P],
                    hT_hi[:, 0:FC - 1].rearrange("p c t -> p (c t)"))
                low(hT_lo[0:FLAST, FC - 1], p_th[0:FLAST, (FC - 1) * P:FC * P],
                    hT_hi[0:FLAST, FC - 1]).then_inc(s_ht, 1)

            def x_lo(t, par):
                dve.wait_ge(s_xth, t + 1)
                low(xT_lo[:, par], xnT[:, :, bass.ds(P * t, P)], xT_hi[:, par]).then_inc(s_xt, 1)

            def shared_out(t, slot, nth):
                dve.wait_ge(s_x[slot], 16 * (nth + 1))
                v.tensor_tensor(xring[:, slot, :], xring[:, slot, :], bias_b[:], ALU.add
                                ).then_inc(s_xbias, 1)
                dve.wait_ge(s_xbias, t + 1)
                dve.wait_ge(s_dd, 2 * t + 2)
                if not isinstance(t, int) or t >= 2:
                    dve.wait_ge(s_sst[slot % 2], 8 * (t - slot % 2))
                v.tensor_tensor(y_sb[slot % 2], p_y[slot % 2][:], xring[:, slot, :], ALU.add
                                ).then_inc(s_ysh, 1)

            def w_lo_T(i, c):
                dve.wait_ge(s_wth, DC * i + c + 1)
                low((w_inT, w_outT)[i][1][:, c, :], p_tx[:], (w_inT, w_outT)[i][0][:, c, :]
                    ).then_inc(s_wT, 1)

            routing = [(softmax_top, top_index), (choices, payload),
                       (lambda: w_lo_T(0, 0), lambda: w_lo_T(0, 1)),
                       (lambda: w_lo_T(0, 2), lambda: (w_lo_T(0, 3), ranks())),
                       (extra_slots, slots),
                       (lambda: choice_slots(range(3)), lambda: choice_slots(range(3, TOPK))),
                       (extra_experts, routed), (None, None)]

            def shared_pair(it, j, parts=(None, None), last=False):
                t = 4 * it + j
                h_hT(2 * t)
                if not last:
                    x_lo(t + 1, 1 - j % 2)
                if not isinstance(it, int) or t >= 1:
                    shared_out(t - 1, (j - 1) % 4, it + (4 if j else 3))
                if parts[0]:
                    parts[0]()
                h_hT(2 * t + 1)
                if parts[1]:
                    parts[1]()

            x_lo(0, 0)
            for j in range(3):
                w_lo_piece(1, j, 3 + j)
            less_max()
            decays()
            dve.wait_ge(s_biasl, 16)
            for i in range(4):
                dve.wait_ge(s_xns[i], 16 * TILES // 4)
            dve.wait_ge(s_xnt, TILES)
            for t, parts in enumerate(routing):
                shared_pair(t // 4, t % 4, parts)
            with dve.Fori(len(routing) // 4, TILES // 4 - 1) as it:
                for j in range(4):
                    shared_pair(it, j)
            for j in range(4):
                shared_pair(TILES // 4 - 1, j, last=(j == 3))
            shared_out(TILES - 1, 3, TILES // 4 + 3)

            def xb_lo(b):
                dve.wait_ge(s_xbh, b + 1)
                low(xb[1], xnT[:, :, b * S:(b + 1) * S], xb[0]).then_inc(s_xb, 1)

            def scans(b):
                for m in range(DC):
                    dve.wait_ge(s_q, DC * b + m + 1)
                    if b >= 1:
                        dve.wait_ge(s_st, DC * b)
                    v.tensor_tensor_scan(scan[:, m, :], dec[:, 1, m:m + 1].to_broadcast([P, S]),
                                         q_sb[m % 2], 0.0, ALU.mult, ALU.add).then_inc(s_sc, 1)
                    if b == 0:
                        w_lo_T(1, m)

            def st_lo(b):
                for m in range(DC):
                    dve.wait_ge(s_sth, DC * b + m + 1)
                    low(st[1][:, m, :], scan[:, m, :], st[0][:, m, :]).then_inc(s_st, 1)

            def base_tile(t):
                dve.wait_ge(s_x[t % 4], 16 * (TILES // 4 * 2 + t // 4 + 1))
                dve.wait_ge(s_out, t + 1)
                if t < 2:
                    dve.wait_ge(s_sst[t], 16 * TILES // 2)
                else:
                    dve.wait_ge(s_bst[t % 2], 16 * (t // 2))
                v.tensor_tensor(y_sb[t % 2], p_y[t % 2][:], xring[:, t % 4, :], ALU.add
                                ).then_inc(s_base, 1)

            xb_lo(0)
            for b in range(B):
                scans(b)
                if b + 1 < B:
                    xb_lo(b + 1)
                if b >= 1:
                    for t in range(TPB):
                        base_tile(TPB * (b - 1) + t)
                st_lo(b)

            dve.wait_ge(s_tabt, 1)
            n = MAINB
            for dst, lo, hi in ((ids[:, 0:n], 0, n), (wts[:, 0:n], n, 2 * n),
                                (ids[:, n:COLS], 2 * n, 2 * n + XMAX),
                                (wts[:, n:COLS], 2 * n + XMAX, 2 * n + 2 * XMAX)):
                v.tensor_copy(dst, p_b[:, lo:hi]).then_inc(s_tab, 1)
            for j in range(TPB):
                base_tile(TILES - TPB + j)
                if j < 3:
                    w_lo_piece(0, j, 6 + j)

            def xt_lo(i, par):
                dve.wait_ge(s_xth, i + TILES + 1)
                low(xT_lo[:, par].rearrange("p c t -> p (c t)"), p_tx[:],
                    xT_hi[:, par].rearrange("p c t -> p (c t)")).then_inc(s_xt, 1)

            def round_(it, last):
                def split(m, j):
                    return m % 2, j, 18 * it + 3 * m + j + 6

                for j in range(STEPS):
                    i = STEPS * it + j
                    middle = j in MIDDLE and not (last and MIDDLE[j][0] == 6)
                    h_hT(i + SHARED, split(*MIDDLE[j]) if middle else None)
                    if not last or j + 2 < STEPS:
                        xt_lo(i + 2, j % 2)
                    if not last or SPLITS[j][0] < 6:
                        w_lo_piece(*split(*SPLITS[j]))

            xt_lo(0, 0)
            xt_lo(1, 1)
            round_(0, False)
            with dve.Fori(1, ROUNDS - 1) as it:
                round_(it, False)
            round_(ROUNDS - 1, True)
            dve.wait_ge(s_route, 1)
            more = dve.value_load(cnt_i[0:1, 0:1], min_val=0, max_val=(XMAX - XMID) // 2)
            with dve.If(more > 0):
                with dve.Fori(0, more) as k:
                    i = 2 * k + MIDB
                    for par in range(2):
                        for j in range(3):
                            w_lo_piece(par, j, 6 * k + 18 * ROUNDS + 6 + 3 * par + j)
                    for j in range(2):
                        xt_lo(i + j, j)
                    for j in range(2):
                        h_hT(i + j + SHARED)


_INS = ("x", "W_in", "W_out", "decay", "bias")
_NAMES = ["L0_attn_" + n for n in _INS] + ["L0_ffn_" + n for n in
                                           ("wg_router", "w_gate", "w_up", "w_down", "ws_gate",
                                            "ws_up", "ws_down")]


def kernel(**inputs):
    import numpy as np
    import concourse.bacc as bacc
    from concourse.bass_utils import run_bass_kernel_spmd

    nc = bacc.Bacc("TRN2", target_bir_lowering=False, num_devices=1)
    arrays, args = {}, []
    for name in _NAMES:
        a = np.ascontiguousarray(inputs[name])
        if name == "L0_attn_x":
            a = a.reshape(T, D)
        arrays[name] = a
        args.append(nc.dram_tensor(name, a.shape, mybir.dt.from_np(a.dtype), kind="ExternalInput").ap())
    out = nc.dram_tensor("out", (ROWS, D), F32, kind="ExternalOutput").ap()
    xn_rows = nc.dram_tensor("xn_rows", (ROWS, D), F32, kind="Internal").ap()
    table = nc.dram_tensor("slot_table", (TABLE + T * E, 2), F32, kind="Internal").ap()
    build(nc, *args, out, xn_rows, table)
    r = run_bass_kernel_spmd(nc, [arrays], core_ids=[0])
    return r.results[0]["out"][0:T].reshape(B, S, D)
```

```python
from contextlib import ExitStack

import concourse.bass as bass
from concourse import mybir

F32 = mybir.dt.float32
F32R = mybir.dt.float32r
BF16 = mybir.dt.bfloat16
I32 = mybir.dt.int32
U32 = mybir.dt.uint32
ALU = mybir.AluOpType
ACT = mybir.ActivationFunctionType
AX = mybir.AxisListType.X

P = 128
B, S, D = 4, 512, 512
T = B * S
TILES = T // P
TPB = S // P
DC = D // P
E, F, TOPK = 32, 352, 6
CAP = 2 * (T * TOPK // E)
FC = 3
FLAST = F - (FC - 1) * P
SHARED = 2 * TILES
EPB = 3
MAINB = E * EPB
XMID = E // 2
XMAX = 64
COLS = MAINB + XMAX
ROWS = T + P
TABLE = COLS * P
GU = DC * F
WW = 2 * GU + FC * D
PIECES = ((0, GU), (GU, 2 * GU), (2 * GU, WW))

ROUNDS = E // 4
LEN = (EPB, EPB, 1, EPB, EPB, 1)
STEPS = sum(LEN)
MIDB = ROUNDS * STEPS
SET_OF = [m for m, n in enumerate(LEN) for _ in range(n)] + [6, 6]
LAST = [sum(LEN[:m + 1]) - 1 for m in range(6)]
SPLITS = [(1, 0), (1, 1), (1, 2), (2, 0), (2, 2), (3, 0), (3, 2),
          (4, 0), (4, 1), (4, 2), (5, 0), (5, 2), (6, 0), (6, 2)]
MIDDLE = {4: (2, 1), 6: (3, 1), 11: (5, 1), 13: (6, 1)}


def table_column(it, j):
    it, j = it + j // STEPS, j % STEPS
    if SET_OF[j] in (2, 5):
        return MAINB + 2 * it + SET_OF[j] // 3
    return 4 * EPB * it + j - SET_OF[j] // 3


def build(nc, x, w_in, w_out, decay, bias, wg, w_gate, w_up, w_down, ws_gate, ws_up, ws_down, out,
          xn_rows, table):
    with ExitStack() as ctx:
        def sb(name, shape, dt=F32):
            return ctx.enter_context(nc.sbuf_tensor(name, shape, dt))

        def ps(name, shape):
            return ctx.enter_context(nc.psum_tensor(name, shape, F32))

        def sem(name):
            return ctx.enter_context(nc.semaphore(name))

        w_hi = sb("w_hi", [P, 2, WW], F32R)
        w_lo = sb("w_lo", [P, 2, WW], F32R)
        raw = sb("raw", [P, 2, WW])
        xnT = sb("xnT", [P, DC, T])
        xring = sb("xring", [P, 4, D])
        rows = sb("rows", [P, 4 * D])
        sg = sb("sg", [P, F])
        h_sb = sb("h_sb", [P, F])
        xT_hi = sb("xT_hi", [P, 2, DC, P], F32R)
        xT_lo = sb("xT_lo", [P, 2, DC, P], F32R)
        hT_hi = sb("hT_hi", [P, FC, P], F32R)
        hT_lo = sb("hT_lo", [P, FC, P], F32R)
        scan = sb("scan", [P, DC, S])
        q_sb = sb("q_sb", [P, 2, S])
        scratch = sb("scratch", [P, 4, TILES * E])
        eq = sb("eq", [P, TOPK, E * TILES], BF16)
        ident = sb("ident", [P, P])
        before = sb("before", [P, P], BF16)
        ones = sb("ones", [P, P], BF16)
        bias_b = sb("bias_b", [P, D])
        wgT = sb("wgT", [P, DC, E])
        dec = sb("dec", [P, 4, DC])
        epst = sb("epst", [P, 1])
        unused = sb("unused", [P, 1])
        stats = sb("stats", [P, 2, 6])
        mv = sb("mv", [P, TILES, 2])
        std = sb("std", [P, TILES])
        rstd = sb("rstd", [P, TILES])
        nmr = sb("nmr", [P, TILES])
        r16 = sb("r16", [P, 6, TILES])
        top8 = sb("top8", [P, TILES, 8])
        idx8 = sb("idx8", [P, TILES, 8], U32)
        idxf = sb("idxf", [P, TILES, 8])
        iota_e = sb("iota_e", [P, E])
        tok_id = sb("tok_id", [P, TILES])
        trash = sb("trash", [P, E])
        e384 = sb("e384", [P, E])
        blk128 = sb("blk128", [P, XMAX])
        r32 = sb("r32", [P, 7, E])
        slot_f = sb("slot_f", [P, TOPK, TILES])
        slot_i = sb("slot_i", [P, TOPK * TILES, 1], I32)
        pay = sb("pay", [P, TOPK * TILES, 2])
        eidf = sb("eidf", [P, XMAX])
        eid = sb("eid", [P, XMAX], I32)
        cnt_i = sb("cnt_i", [P, 4], I32)
        tabrow = sb("tabrow", [P, 2, 2 * P])
        ids = sb("ids", [P, COLS], I32)
        wts = sb("wts", [P, COLS])
        gidx = sb("gidx", [P, 2], I32)
        sidx = sb("sidx", [P, 2], I32)
        swt = sb("swt", [P, 2])
        ridx = sb("ridx", [P, 8], I32)
        rpay = sb("rpay", [P, 8, 2])

        xe = [rows[:, i * D:(i + 1) * D] for i in range(2)]
        y_sb = [rows[:, (2 + i) * D:(3 + i) * D] for i in range(2)]
        half = DC * D
        xb = [w[:, 0, 0:half].rearrange("p (c t) -> p c t", c=DC) for w in (w_hi, w_lo)]
        w_inT = [w[:, 0, half:2 * half].rearrange("p (c e) -> p c e", c=DC) for w in (w_hi, w_lo)]
        st = [w[:, 1, 0:half].rearrange("p (c t) -> p c t", c=DC) for w in (w_hi, w_lo)]
        w_outT = [w[:, 1, half:2 * half].rearrange("p (c e) -> p c e", c=DC) for w in (w_hi, w_lo)]
        nat = [raw[:, 0, i * half:(i + 1) * half].rearrange("p (j d) -> p j d", j=DC) for i in range(2)]
        TE = TILES * E
        ra, rb, rc, reset = (scratch[:, i, :] for i in range(4))
        first = [raw[:, 1, t * D:(t + 1) * D] for t in range(4)]
        wg_nat = ra[0:E, :]

        p_tx = ps("p_tx", [P, 512])
        p_th = ps("p_th", [P, 512])
        p_g = ps("p_g", [P, 512])
        p_u = ps("p_u", [P, 512])
        p_y = [ps(f"p_y{i}", [P, 512]) for i in range(2)]
        p_a = ps("p_a", [P, 512])
        p_b = ps("p_b", [P, 512])
        p_gu = [p_g, p_u]

        s_x = [sem(f"x_loaded{i}") for i in range(4)]
        s_x0 = [sem(f"x_first_loaded{i}") for i in range(4)]
        s_wgl = sem("wg_loaded")
        s_decl = sem("decay_loaded")
        s_nat = [sem(f"nat_loaded{i}") for i in range(2)]
        s_biasl = sem("bias_loaded")
        s_xbias = sem("x_plus_bias_ready")
        s_ident = sem("ident_ready")
        s_const = sem("consts_ready")
        s_pool0 = sem("pool_setup_chain")
        s_zero = sem("zero_rows_stored")
        s_pre = sem("table_prefilled")
        s_rawz = sem("raw_tail_set")
        s_eps = sem("eps_ready")
        s_var = sem("variance_ready")
        s_std = sem("std_ready")
        s_norm = sem("norm_factors_ready")
        s_xn = sem("xn_ready")
        s_xns = [sem(f"xn_stored{i}") for i in range(4)]
        s_xnt = sem("xn_transposed")
        s_xnT = sem("xnT_ready")
        s_wgt = sem("wg_transposed")
        s_wgT = sem("wgT_ready")
        s_wt = sem("w_transposed")
        s_wth = sem("wT_hi_ready")
        s_wT = sem("wT_ready")
        s_dec = sem("decay_chain")
        s_dece = sem("decay_exp")
        s_lg = sem("logits_ready")
        s_ch = sem("dve_chain")
        s_lgm = sem("logits_less_max")
        s_ex = sem("logits_exp")
        s_eq = sem("choices_ready")
        s_cn = sem("counts_ready")
        s_reset = sem("reset_ready")
        s_slots = sem("slots_ready")
        s_route = sem("extra_blocks_ready")
        s_xbh = sem("xb_hi_ready")
        s_xb = sem("xb_ready")
        s_in = sem("in_projected")
        s_q = sem("q_ready")
        s_sc = sem("scanned")
        s_sth = sem("states_hi_ready")
        s_st = sem("states_ready")
        s_out = sem("out_projected")
        s_base = sem("base_ready")
        s_bst0 = sem("first_bases_stored")
        s_bst = [sem(f"base_stored{i}") for i in range(2)]
        s_ysh = sem("shared_y_ready")
        s_sst = [sem(f"shared_y_stored{i}") for i in range(2)]
        s_ld = [[sem(f"raw_loaded_{'gud'[j]}{i}") for i in range(2)] for j in range(3)]
        s_wh = sem("weights_hi_ready")
        s_w = sem("weights_split")
        s_gi = sem("gather_index_staged")
        s_gat = [sem(f"gathered{i}") for i in range(2)]
        s_stg = sem("scatter_index_staged")
        s_scat = sem("scattered")
        s_turn = sem("pool_turn")
        s_ri = sem("route_entry_staged")
        s_rd = [sem(f"route_entries_stored{i}") for i in range(2)]
        s_tabl = sem("table_loaded")
        s_tabt = sem("table_transposed")
        s_tab = sem("table_ready")
        s_tx = sem("x_transposed")
        s_xth = sem("xT_hi_ready")
        s_xt = sem("xT_ready")
        s_gd = sem("gate_done")
        s_ud = sem("up_done")
        s_sg = sem("silu_ready")
        s_h = sem("h_ready")
        s_th = sem("h_transposed")
        s_hth = sem("hT_hi_ready")
        s_ht = sem("hT_ready")
        s_dd = sem("down_done")
        s_y = sem("y_ready")

        block = ctx.enter_context(nc.Block())

        BASES = (TILES - 4) // 2

        def x_tile(t):
            return first[t] if t < 4 else xring[:, t % 4, :]

        def loaded(j, nth):
            return (2 if j == 2 else 1) * 16 * (nth + 1)

        @block.sync
        def _(sp):
            def load_tile(slot, src):
                sp.dma_start(xring[:, slot, :], src).then_inc(s_x[slot], 16)

            def tile_rows(dram, t):
                return dram[bass.ds(P * t, P), :]

            def load_set(par, wait, g_src, u_src, d_src):
                for j, src in ((0, g_src), (1, u_src)):
                    if wait is not None:
                        sp.wait_ge(s_w, wait + j + 1)
                    lo, hi = PIECES[j]
                    sp.dma_start(raw[:, par, lo:hi].rearrange("p (c f) -> p c f", c=DC), src
                                 ).then_inc(s_ld[j][par], 16)
                if wait is not None:
                    sp.wait_ge(s_w, wait + 3)
                lo, hi = PIECES[2]
                full = (FC - 1) * P
                sp.dma_start(raw[:, par, lo:hi - D].rearrange("p (c d) -> p c d", d=D),
                             d_src(0, full).rearrange("(c p) d -> p c d", p=P)).then_inc(s_ld[2][par], 16)
                sp.dma_start(raw[0:FLAST, par, hi - D:hi], d_src(full, F)).then_inc(s_ld[2][par], 16)

            def shared_set(s):
                load_set(s, None,
                         ws_gate.rearrange("(p c) f -> p c f", c=DC)[:, :, s * F:(s + 1) * F],
                         ws_up.rearrange("(p c) f -> p c f", c=DC)[:, :, s * F:(s + 1) * F],
                         lambda a, z: ws_down[s * F + a:s * F + z, :])

            def expert_set(par, wait, e):
                load_set(par, wait,
                         w_gate[e].rearrange("(p c) f -> p c f", c=DC),
                         w_up[e].rearrange("(p c) f -> p c f", c=DC),
                         lambda a, z: w_down[e][a:z, :])

            def extra_set(par, wait, k):
                e = sp.value_load(eid[0:1, bass.ds(k, 1)], min_val=0, max_val=E - 1)
                expert_set(par, wait, e)

            def store_xn(t):
                sp.wait_ge(s_xn, t + 1)
                sp.dma_start(tile_rows(xn_rows, t), rows[:, (t % 4) * D:(t % 4 + 1) * D]
                             ).then_inc(s_xns[t % 4], 16)

            for t in range(4):
                sp.dma_start(first[t], tile_rows(x, t)).then_inc(s_x0[t], 16)
            for t in range(4, 8):
                load_tile(t % 4, tile_rows(x, t))
            for t in range(4):
                store_xn(t)
            for t in range(8, TILES):
                sp.wait_ge(s_xn, t - 3)
                load_tile(t % 4, tile_rows(x, t))
                store_xn(t - 4)

            for t in range(4):
                sp.wait_ge(s_base, t + 1)
                sp.dma_start(tile_rows(out, t), first[t]).then_inc(s_bst0, 16)
            for t in range(TILES - 4, TILES):
                store_xn(t)
            for t in range(4, 8):
                load_tile(t % 4, tile_rows(x, t))
            sp.wait_ge(s_wt, 2 * DC)
            shared_set(0)
            sp.wait_ge(s_rawz, 2)
            sp.wait_ge(s_bst0, 64)
            shared_set(1)

            def store_base(t, j):
                sp.wait_ge(s_base, t + 1)
                sp.dma_start(tile_rows(out, t), y_sb[j % 2]).then_inc(s_bst[j % 2], 16)

            with sp.Fori(1, 3) as it:
                for j in range(4):
                    store_base(4 * it + j, j)
                    load_tile(j, tile_rows(x, 4 * it + 4 + j))
            for t in range(TILES - 4, TILES):
                store_base(t, t % 4)

            for i in range(2):
                sp.wait_ge(s_bst[i], 16 * BASES)
            for t in range(4):
                load_tile(t, tile_rows(out, t))

            def store_shared(t, j):
                sp.wait_ge(s_ysh, t + 1)
                sp.dma_start(tile_rows(out, t), y_sb[j % 2]).then_inc(s_sst[j % 2], 16)

            expert_set(0, 0, 0)
            expert_set(1, 3, 1)
            with sp.Fori(0, 3) as it:
                for j in range(4):
                    store_shared(4 * it + j, j)
                    load_tile(j, tile_rows(out, 4 * it + 4 + j))
            for t in range(TILES - 4, TILES - 1):
                store_shared(t, t % 4)

            sp.wait_ge(s_route, 1)

            def round_sets(it, sets):
                for m in sets:
                    wait = 18 * it + 3 * m
                    if m in (2, 5):
                        extra_set(m % 2, wait, 2 * it + m // 3)
                    else:
                        expert_set(m % 2, wait, 4 * it + (0, 1, 0, 2, 3)[m])

            round_sets(0, [2])
            store_shared(TILES - 1, 3)
            round_sets(0, range(3, 6))
            with sp.Fori(1, ROUNDS) as it:
                round_sets(it, range(6))
            more = sp.value_load(cnt_i[0:1, 0:1], min_val=0, max_val=(XMAX - XMID) // 2)
            with sp.If(more > 0):
                with sp.Fori(0, more) as k:
                    for par in range(2):
                        extra_set(par, 6 * k + 3 * (6 * ROUNDS + par), 2 * k + XMID + par)

        @block.gpsimd
        def _(pool):
            g = nc.gpsimd
            zrow = scan[:, 0, :]
            g.memset(ident[:], 0.0).then_inc(s_pool0, 1)
            pool.wait_ge(s_pool0, 1)
            g.affine_select(out=ident[:], in_=ident[:], compare_op=ALU.not_equal, fill=1.0, base=0,
                            pattern=[[-1, P]], channel_multiplier=1).then_inc(s_ident, 1)
            g.memset(zrow, 0.0).then_inc(s_pool0, 1)
            g.memset(raw[:, 0, WW - D:WW], 0.0).then_inc(s_rawz, 1)
            g.memset(raw[:, 1, WW - D:WW], 0.0).then_inc(s_rawz, 1)
            pool.wait_ge(s_pool0, 2)
            for dst in (xn_rows, out):
                pool.dma_start(dst[T:ROWS, :], zrow).then_inc(s_zero, 16)
            tr = tabrow[:, 0, :].rearrange("p (s two) -> p s two", two=2)
            g.memset(tabrow[:, 0, :], 0.0).then_inc(s_pool0, 1)
            pool.wait_ge(s_pool0, 3)
            g.iota(tr[:, :, 0], pattern=[[1, P]], base=T, channel_multiplier=0,
                   allow_small_or_imprecise_dtypes=True).then_inc(s_pool0, 1)
            pool.wait_ge(s_pool0, 4)
            tb = table[0:TABLE, :].rearrange("(b s) two -> b (s two)", s=P)
            pool.dma_start(tb[0:P, :], tabrow[:, 0, :]).then_inc(s_pre, 16)
            pool.dma_start(tb[P:COLS, :], tabrow[0:COLS - P, 0, :]).then_inc(s_pre, 16)

            def io(ap, pattern, base, mult):
                g.iota(ap, pattern=pattern, base=base, channel_multiplier=mult,
                       allow_small_or_imprecise_dtypes=True).then_inc(s_const, 1)

            io(iota_e[:], [[1, E]], 0, 0)
            io(tok_id[:], [[P, TILES]], 0, 1)
            io(trash[:], [[T, E]], TABLE, 0)
            io(e384[:], [[EPB * P, E]], 0, 0)
            io(blk128[:], [[P, XMAX]], 0, 0)
            g.memset(ones[:], 1.0).then_inc(s_const, 1)
            g.memset(before[:], 1.0).then_inc(s_const, 1)
            pool.wait_ge(s_const, 7)
            g.affine_select(out=before[:], in_=before[:], compare_op=ALU.is_gt, fill=0.0, base=0,
                            pattern=[[1, P]], channel_multiplier=-1).then_inc(s_const, 1)
            g.memset(reset, 1.0).then_inc(s_reset, 1)
            pool.wait_ge(s_reset, 1)
            g.memset(reset.rearrange("p (e i) -> p e i", i=TILES)[:, :, 0:1], 0.0).then_inc(s_reset, 1)

            def wait(semaphore, value):
                pool.wait_ge(semaphore, value)
                pool.sem_inc(s_turn, 1)

            def route(four, stage_, left):
                if left is not None:
                    wait(s_rd[stage_], left)
                own = slice(4 * stage_, 4 * stage_ + 4)
                g.tensor_copy(ridx[:, own], slot_i[:, bass.ds(4 * four, 4), 0]).then_inc(s_ri, 1)
                g.tensor_copy(rpay[:, own, :], pay[:, bass.ds(4 * four, 4), :]).then_inc(s_ri, 1)
                wait(s_ri, 2 * four + 2)
                for c in range(4 * stage_, 4 * stage_ + 4):
                    pool.indirect_dma_start(
                        out=table[:, :], in_=rpay[:, c, :], in_offset=None,
                        out_offset=bass.IndirectOffsetOnAxis(ap=ridx[:, c:c + 1], axis=0),
                        bounds_check=TABLE + T * E - 1).then_inc(s_rd[stage_], 16)

            entries = TOPK * TILES
            pool.wait_ge(s_slots, 1)
            pool.wait_ge(s_pre, 32)
            route(0, 0, None)
            route(1, 1, None)
            with pool.Fori(1, entries // 8) as it:
                for i in range(2):
                    route(2 * it + i, i, 64 * it)
            for i in range(2):
                pool.wait_ge(s_rd[i], 8 * entries)
            pool.dma_start(tabrow[0:MAINB, 0, :], tb[0:MAINB, :]).then_inc(s_tabl, 16)
            pool.dma_start(tabrow[0:XMAX, 1, :], tb[MAINB:COLS, :]).then_inc(s_tabl, 16)

            def gather(i, par, col):
                g.tensor_copy(gidx[:, par:par + 1], ids[:, bass.ds(col, 1)]).then_inc(s_gi, 1)
                wait(s_gi, i + 1)
                pool.indirect_dma_start(
                    out=xe[par], out_offset=None, in_=xn_rows[:, :],
                    in_offset=bass.IndirectOffsetOnAxis(ap=gidx[:, par:par + 1], axis=0),
                    bounds_check=ROWS - 1).then_inc(s_gat[par], 16)

            def stage(par, col):
                g.tensor_copy(sidx[:, par:par + 1], ids[:, bass.ds(col, 1)]).then_inc(s_stg, 1)
                g.tensor_copy(swt[:, par:par + 1], wts[:, bass.ds(col, 1)]).then_inc(s_stg, 1)

            def scatter(i, par):
                if isinstance(i, int) and i == 0:
                    for k in range(2):
                        pool.wait_ge(s_sst[k], 16 * TILES // 2)
                pool.wait_ge(s_y, i + 1)
                wait(s_stg, 2 * i + 2)
                pool.indirect_dma_start(
                    out=out[:, :], in_=y_sb[par], in_offset=None,
                    out_offset=bass.IndirectOffsetOnAxis(ap=sidx[:, par:par + 1], axis=0),
                    bounds_check=ROWS - 1, compute_op=ALU.add).then_inc(s_scat, 16)

            def step(i, par, col, col3):
                if col3 is not None:
                    wait(s_tx, i + 2)
                    gather(i + 3, 1 - par, col3)
                if not isinstance(i, int) or i >= 2:
                    wait(s_scat, 16 * (i - 1))
                stage(par, col)
                if not isinstance(i, int) or i >= 1:
                    scatter(i - 1, 1 - par)

            def columns(it, j):
                over = isinstance(it, int) and it == ROUNDS - 1 and j + 3 >= STEPS
                return table_column(it, j), None if over else table_column(it, j + 3)

            pool.wait_ge(s_tab, 4)
            pool.wait_ge(s_zero, 32)
            for i in range(4):
                pool.wait_ge(s_xns[i], 16 * TILES // 4)
            gather(0, 0, 0)
            gather(1, 1, 1)
            pool.wait_ge(s_tx, 1)
            gather(2, 0, 2)
            for j in range(STEPS):
                step(j, j % 2, *columns(0, j))
            with pool.Fori(1, ROUNDS - 1) as it:
                for j in range(STEPS):
                    step(STEPS * it + j, j % 2, *columns(it, j))
            for j in range(STEPS):
                step(MIDB - STEPS + j, j % 2, *columns(ROUNDS - 1, j))
            wait(s_scat, 16 * (MIDB - 1))
            scatter(MIDB - 1, 1)
            pool.wait_ge(s_scat, 16 * MIDB)
            more = pool.value_load(cnt_i[0:1, 0:1], min_val=0, max_val=(XMAX - XMID) // 2)
            with pool.If(more > 0):
                with pool.Fori(0, more) as k:
                    i, col = 2 * k + MIDB, 2 * k + MAINB + XMID
                    for j in range(2):
                        wait(s_tx, i)
                        gather(i + j, j, col + j)
                    for j in range(2):
                        stage(j, col + j)
                    for j in range(2):
                        scatter(i + j, j)
                        wait(s_scat, 16 * (i + j + 1))

        @block.scalar
        def _(act):
            a = nc.scalar
            act.dma_start(wg_nat, wg).then_inc(s_wgl, 16)
            act.dma_start(dec[:, 0, :], decay.rearrange("(p m) -> p m", m=DC)).then_inc(s_decl, 16)
            act.dma_start(bias_b[:], bias.rearrange("(a n) -> a n", a=1).to_broadcast([P, D])
                          ).then_inc(s_biasl, 16)
            act.wait_ge(s_rawz, 1)
            for i, w in ((0, w_in), (1, w_out)):
                act.dma_start(nat[i], w.rearrange("(j p) d -> p j d", p=P)).then_inc(s_nat[i], 16)

            def copy(dst, src, scale=1.0):
                return a.activation(dst, src, ACT.Copy, scale=scale)

            def w_hi_piece(par, j, ld, free=None):
                act.wait_ge(s_ld[j][par], ld)
                if free is not None:
                    act.wait_ge(s_dd if j == 2 else s_ud, free)
                lo, hi = PIECES[j]
                copy(w_hi[:, par, lo:hi], raw[:, par, lo:hi]).then_inc(s_wh, 1)

            def normalise(t):
                act.wait_ge(s_var, t // 2 + 1)
                a.activation(std[:, t:t + 2], mv[:, t:t + 2, 1], ACT.Sqrt, bias=epst[:]
                             ).then_inc(s_std, 1)
                act.wait_ge(s_norm, t // 2 + 1)
                for t in (t, t + 1):
                    if t >= 4:
                        act.wait_ge(s_xns[t % 4], 16 * (t // 4))
                        act.wait_ge(s_xnt, t - 3)
                    a.activation(rows[:, (t % 4) * D:(t % 4 + 1) * D], x_tile(t),
                                 ACT.Identity, scale=rstd[:, t:t + 1], bias=nmr[:, t:t + 1]
                                 ).then_inc(s_xn, 1)

            def x_hi(t, par):
                act.wait_ge(s_xnT, TILES)
                copy(xT_hi[:, par], xnT[:, :, bass.ds(P * t, P)]).then_inc(s_xth, 1)

            def silu_hT(b, y=None, piece=None):
                act.wait_ge(s_gd, b + 1)
                a.activation(sg[:], p_g[:, 0:F], ACT.Silu).then_inc(s_sg, 1)
                if piece is not None:
                    w_hi_piece(*piece)
                if y is not None:
                    y_out(*y)
                act.wait_ge(s_th, b + 1)
                copy(hT_hi[:, 0:FC - 1].rearrange("p c t -> p (c t)"), p_th[:, 0:(FC - 1) * P])
                copy(hT_hi[0:FLAST, FC - 1], p_th[0:FLAST, (FC - 1) * P:FC * P]).then_inc(s_hth, 1)

            def wT_hi(i, c):
                act.wait_ge(s_wt, DC * i + c + 1)
                copy((w_inT, w_outT)[i][0][:, c, :], p_y[c % 2][:]).then_inc(s_wth, 1)

            def xb_hi(b):
                act.wait_ge(s_xnT, TPB * (b + 1))
                if b >= 1:
                    act.wait_ge(s_in, DC * b)
                copy(xb[0], xnT[:, :, b * S:(b + 1) * S]).then_inc(s_xbh, 1)

            def q(b, chunks=range(DC)):
                for m in chunks:
                    act.wait_ge(s_in, DC * b + m + 1)
                    if DC * b + m >= 2:
                        act.wait_ge(s_sc, DC * b + m - 1)
                    copy(q_sb[:, m % 2], p_gu[m % 2][:], scale=dec[:, 3, m:m + 1]).then_inc(s_q, 1)

            def st_hi(b):
                for m in range(DC):
                    act.wait_ge(s_sc, DC * b + m + 1)
                    if b >= 1:
                        act.wait_ge(s_out, TPB * b)
                    copy(st[0][:, m, :], scan[:, m, :]).then_inc(s_sth, 1)

            act.wait_ge(s_eps, 1)
            a.activation(unused[:], epst[:], ACT.Sqrt, bias=epst[:])
            normalise(0)
            normalise(2)
            wT_hi(0, 0)
            wT_hi(0, 1)
            xb_hi(0)
            wT_hi(0, 2)
            wT_hi(0, 3)
            act.wait_ge(s_decl, 16)
            a.activation(dec[:, 1, :], dec[:, 0, :], ACT.Exp, scale=-1.0).then_inc(s_dece, 1)
            normalise(4)
            normalise(6)
            act.wait_ge(s_dec, 3)
            for b in range(2):
                q(b, [0])
                wT_hi(1, 2 * b)
                wT_hi(1, 2 * b + 1)
                q(b, [1])
                normalise(4 * b + 8)
                q(b, [2])
                normalise(4 * b + 10)
                q(b, [3])
                if b == 0:
                    xb_hi(1)
                    st_hi(0)
            xb_hi(2)
            act.wait_ge(s_lgm, 1)
            a.activation(rb, ra, ACT.Exp).then_inc(s_ex, 1)
            st_hi(1)
            q(2)
            xb_hi(3)
            st_hi(2)
            q(3)
            act.wait_ge(s_in, DC * B)
            w_hi_piece(0, 0, loaded(0, 0))
            w_hi_piece(0, 1, loaded(1, 0))
            x_hi(0, 0)
            w_hi_piece(0, 2, loaded(2, 0))
            st_hi(3)
            silu_hT(0)
            x_hi(1, 1)
            act.wait_ge(s_out, TILES)
            for j in range(3):
                w_hi_piece(1, j, loaded(j, 0))

            def xt_hi(i, par):
                act.wait_ge(s_tx, i + 1)
                copy(xT_hi[:, par].rearrange("p c t -> p (c t)"), p_tx[:]).then_inc(s_xth, 1)

            def shared_pair(t, par):
                silu_hT(2 * t)
                x_hi(t + 1, 1 - par)
                silu_hT(2 * t + 1)

            silu_hT(1)
            with act.Fori(0, TILES // 2 - 1) as it:
                for j in range(2):
                    shared_pair(2 * it + 1 + j, 1 - j)
            silu_hT(SHARED - 2)
            xt_hi(0, 0)
            w_hi_piece(0, 0, loaded(0, 1), SHARED - 1)
            silu_hT(SHARED - 1, piece=(0, 1, loaded(1, 1), SHARED - 1))

            def y_out(i, par):
                act.wait_ge(s_dd, i + SHARED + 1)
                act.wait_ge(s_stg, 2 * i + 2)
                if isinstance(i, int) and i < 2:
                    act.wait_ge(s_sst[i], 16 * TILES // 2)
                copy(y_sb[par], p_y[par][:], scale=swt[:, par:par + 1]).then_inc(s_y, 1)

            def round_(it, first, last):
                def split(m, j):
                    nth = 3 * it + m // 2 + 1
                    free = STEPS * it + (LAST[m - 2] if m >= 2 else LAST[m - 2] - STEPS)
                    return m % 2, j, (2 if j == 2 else 1) * 16 * (nth + 1), free + SHARED + 1

                for j in range(STEPS):
                    i = STEPS * it + j
                    middle = j in MIDDLE and not (last and MIDDLE[j][0] == 6)
                    silu_hT(i + SHARED, None if first and j == 0 else (i - 1, 1 - j % 2),
                            split(*MIDDLE[j]) if middle else None)
                    if not last or j + 2 < STEPS:
                        xt_hi(i + 2, j % 2)
                    if not last or SPLITS[j][0] < 6:
                        w_hi_piece(*split(*SPLITS[j]))

            xt_hi(1, 1)
            w_hi_piece(0, 2, loaded(2, 1), SHARED - 1)
            round_(0, True, False)
            with act.Fori(1, ROUNDS - 1) as it:
                round_(it, False, False)
            round_(ROUNDS - 1, False, True)
            y_out(MIDB - 1, 1)
            more = act.value_load(cnt_i[0:1, 0:1], min_val=0, max_val=(XMAX - XMID) // 2)
            with act.If(more > 0):
                with act.Fori(0, more) as k:
                    i = 2 * k + MIDB
                    for par in range(2):
                        for j in range(3):
                            w_hi_piece(par, j, (2 if j == 2 else 1) * 16 * (k + 3 * ROUNDS + 2),
                                       i + SHARED)
                    for j in range(2):
                        xt_hi(i + j, j)
                    silu_hT(i + SHARED)
                    silu_hT(i + SHARED + 1, (i, 0))
                    y_out(i + 1, 1)

        @block.tensor
        def _(pe):
            t_ = nc.tensor
            pe.wait_ge(s_ident, 1)
            pe.wait_ge(s_wgl, 16)
            for c in range(DC):
                last = t_.transpose(p_b[:, c * E:(c + 1) * E], wg_nat[:, c::DC], ident[0:E, 0:E])
            last.then_inc(s_wgt, 1)

            def tile_T(t):
                pe.wait_ge(s_xn, t + 1)
                if t >= 2:
                    pe.wait_ge(s_xnT, t - 1)
                for c in range(DC):
                    last = t_.transpose((p_tx, p_th)[t % 2][:, c * P:(c + 1) * P],
                                        rows[:, (t % 4) * D + c:(t % 4 + 1) * D:DC], ident[:])
                last.then_inc(s_xnt, 1)

            def logits(t):
                pe.wait_ge(s_xnT, t + 1)
                if t == 0:
                    pe.wait_ge(s_wgT, 1)
                for c in range(DC):
                    last = t_.matmul(p_a[:, t * E:(t + 1) * E], xnT[:, c, t * P:(t + 1) * P],
                                     wgT[:, c, :], start=(c == 0), stop=(c == DC - 1))
                last.then_inc(s_lg, 1)

            def w_T(i, c):
                pe.wait_ge(s_nat[i], 16)
                if DC * i + c >= 2:
                    pe.wait_ge(s_wT, DC * i + c - 1)
                for j in range(DC):
                    last = t_.transpose(p_y[c % 2][:, j * P:(j + 1) * P], nat[i][:, j, c::DC], ident[:])
                last.then_inc(s_wt, 1)

            def three(dst, stat, mov, first, last):
                t_.matmul(dst, stat[0], mov[0], start=first, stop=False)
                t_.matmul(dst, stat[0], mov[1], start=False, stop=False)
                return t_.matmul(dst, stat[1], mov[0], start=False, stop=last)

            def up(x_ready, xpar, par, pieces):
                pe.wait_ge(s_xt, x_ready)
                for j, dst, done in ((0, p_g, s_gd), (1, p_u, s_ud)):
                    pe.wait_ge(s_w, pieces + 1 + j)
                    for c in range(DC):
                        lo = PIECES[j][0] + c * F
                        mm = three(dst[:, 0:F], [v[:, xpar, c, :] for v in (xT_hi, xT_lo)],
                                   [w[:, par, lo:lo + F] for w in (w_hi, w_lo)], c == 0, c == DC - 1)
                    mm.then_inc(done, 1)

            def down(b, bank, par, pieces, first=True, last=True):
                pe.wait_ge(s_ht, b + 1)
                pe.wait_ge(s_w, pieces + 3)
                for c in range(FC):
                    k = P if c < FC - 1 else FLAST
                    lo = PIECES[2][0] + c * D
                    mm = three(p_y[bank][:], [v[0:k, c, :] for v in (hT_hi, hT_lo)],
                               [w[0:k, par, lo:lo + D] for w in (w_hi, w_lo)],
                               first and c == 0, last and c == FC - 1)
                mm.then_inc(s_dd, 1)

            def h_T(b):
                pe.wait_ge(s_h, b + 1)
                for c in range(FC):
                    k = P if c < FC - 1 else FLAST
                    mm = t_.transpose(p_th[0:k, c * P:(c + 1) * P], h_sb[:, c * P:c * P + k], ident[:])
                mm.then_inc(s_th, 1)

            def counts():
                pe.wait_ge(s_eq, 1)
                for dst, w in ((p_a, before), (p_b, ones)):
                    for k in range(TOPK):
                        last = t_.matmul(dst[:], w[:], eq[:, k, :], start=(k == 0), stop=(k == TOPK - 1))
                last.then_inc(s_cn, 1)

            def in_proj(b, tiles=()):
                pe.wait_ge(s_xb, b + 1)
                for m in range(DC):
                    if not isinstance(b, int) or DC * b + m >= 2:
                        pe.wait_ge(s_q, DC * b + m - 1)
                    for c in range(DC):
                        mm = three(p_gu[m % 2][:], [w[:, c, m::DC] for w in w_inT],
                                   [v[:, c, :] for v in xb], c == 0, c == DC - 1)
                    mm.then_inc(s_in, 1)
                    if tiles and m == 0:
                        w_T(1, 2 * b)
                        w_T(1, 2 * b + 1)
                    elif tiles and m <= 2:
                        tile_T(tiles[2 * m - 2])
                        tile_T(tiles[2 * m - 1])

            def out_proj(b, tiles=range(TPB)):
                pe.wait_ge(s_st, DC * b + DC)
                for t in tiles:
                    if TPB * b + t >= 2:
                        pe.wait_ge(s_base, TPB * b + t - 1)
                    for m in range(DC):
                        mm = three(p_y[t % 2][:], [v[:, m, t * P:(t + 1) * P] for v in st],
                                   [w[:, m, :] for w in w_outT], m == 0, m == DC - 1)
                    mm.then_inc(s_out, 1)

            for t in range(4):
                tile_T(t)
            w_T(0, 0)
            w_T(0, 1)
            logits(0)
            w_T(0, 2)
            w_T(0, 3)
            logits(1)
            logits(2)
            pe.wait_ge(s_wT, DC)
            in_proj(0, range(4, 8))
            for t in range(3, 8):
                logits(t)
            in_proj(1, range(8, 12))
            for t in (8, 10):
                logits(t)
                logits(t + 1)
                tile_T(t + 4)
                tile_T(t + 5)
            for t in range(12, TILES):
                logits(t)
            pe.wait_ge(s_wT, 2 * DC)
            out_proj(0)
            in_proj(2)
            out_proj(1)
            counts()
            in_proj(3)
            out_proj(2)
            pe.wait_ge(s_q, DC * B)
            up(1, 0, 0, 0)
            out_proj(3, range(2))
            h_T(0)
            out_proj(3, range(2, TPB))

            def shared_tile(t, par, table=False):
                down(2 * t - 1, 1 - par, 1, 3, first=False)
                h_T(2 * t)
                up(t + 1, par, 1, 3)
                if not isinstance(t, int) or t >= 2:
                    pe.wait_ge(s_ysh, t - 1)
                else:
                    pe.wait_ge(s_base, TILES)
                down(2 * t, par, 0, 0, last=False)
                h_T(2 * t + 1)
                if table:
                    table_T()
                up(t + 2, 1 - par, 0, 0)

            pe.wait_ge(s_base, TILES - 1)
            down(0, 0, 0, 0, last=False)
            up(1, 0, 1, 3)
            h_T(1)
            up(2, 1, 0, 0)
            shared_tile(1, 1)
            with pe.Fori(1, TILES // 2 - 1) as it:
                for j in range(2):
                    shared_tile(2 * it + j, j)

            def table_T():
                pe.wait_ge(s_tabl, 32)
                for w in range(2):
                    t_.transpose(p_b[:, w * MAINB:(w + 1) * MAINB], tabrow[0:MAINB, 0, w::2],
                                 ident[0:MAINB, 0:MAINB])
                    last = t_.transpose(p_b[:, 2 * MAINB + w * XMAX:2 * MAINB + (w + 1) * XMAX],
                                        tabrow[0:XMAX, 1, w::2], ident[0:XMAX, 0:XMAX])
                last.then_inc(s_tabt, 1)

            def x_T(i, par, gathered):
                pe.wait_ge(s_gat[par], gathered)
                pe.wait_ge(s_xt, i + TILES)
                for c in range(DC):
                    last = t_.transpose(p_tx[:, c * P:(c + 1) * P], xe[par][:, c::DC], ident[:])
                last.then_inc(s_tx, 1)

            def round_(it, first, last):
                for j in range(STEPS):
                    i = STEPS * it + j
                    if not first or j >= 1:
                        m = SET_OF[j - 1] if j else -1
                        if first and j <= 2:
                            pe.wait_ge(s_ysh, TILES - 2 + j)
                        if not first or j >= 2:
                            pe.wait_ge(s_y, i - 1)
                        down(i + SHARED - 1, 1 - j % 2, m % 2, 18 * it + 3 * m + 6)
                    h_T(i + SHARED)
                    if not last or j + 2 < STEPS:
                        x_T(i + 2, j % 2, 16 * (STEPS // 2 * it + j // 2 + 2))
                    if not last or j + 1 < STEPS:
                        m = SET_OF[j + 1]
                        up(i + 2 + TILES, 1 - j % 2, m % 2, 18 * it + 3 * m + 6)

            shared_tile(TILES - 2, 0, table=True)
            down(SHARED - 3, 0, 1, 3, first=False)
            h_T(SHARED - 2)
            x_T(0, 0, 16)
            up(TILES, 1, 1, 3)
            pe.wait_ge(s_ysh, TILES - 2)
            down(SHARED - 2, 1, 0, 0, last=False)
            h_T(SHARED - 1)
            x_T(1, 1, 16)
            up(1 + TILES, 0, 0, 6)
            down(SHARED - 1, 1, 1, 3, first=False)
            round_(0, True, False)
            with pe.Fori(1, ROUNDS - 1) as it:
                round_(it, False, False)
            round_(ROUNDS - 1, False, True)
            pe.wait_ge(s_y, MIDB - 1)
            down(MIDB - 1 + SHARED, 1, 1, 18 * ROUNDS + 3)
            pe.wait_ge(s_route, 1)
            more = pe.value_load(cnt_i[0:1, 0:1], min_val=0, max_val=(XMAX - XMID) // 2)
            with pe.If(more > 0):
                with pe.Fori(0, more) as k:
                    i = 2 * k + MIDB
                    n3 = 6 * k + 18 * ROUNDS + 6
                    for j in range(2):
                        x_T(i + j, j, 16 * (k + MIDB // 2 + 1))
                    up(i + TILES + 1, 0, 0, n3)
                    h_T(i + SHARED)
                    up(i + TILES + 2, 1, 1, n3 + 3)
                    pe.wait_ge(s_y, i)
                    down(i + SHARED, 0, 0, n3)
                    h_T(i + SHARED + 1)
                    down(i + SHARED + 1, 1, 1, n3 + 3)

        @block.vector
        def _(dve):
            v = nc.vector
            chain = [0]

            def link(ins):
                chain[0] += 1
                ins.then_inc(s_ch, 1)
                dve.wait_ge(s_ch, chain[0])

            def low(dst, src, hi):
                return v.tensor_tensor(dst, src, hi, ALU.subtract)

            def w_lo_piece(par, j, nth):
                dve.wait_ge(s_wh, nth + 1)
                lo, hi = PIECES[j]
                low(w_lo[:, par, lo:hi], raw[:, par, lo:hi], w_hi[:, par, lo:hi]).then_inc(s_w, 1)

            v.memset(epst[:], 1e-5).then_inc(s_eps, 1)

            def tile_evac(t):
                dve.wait_ge(s_xnt, t + 1)
                v.tensor_copy(xnT[:, :, t * P:(t + 1) * P],
                              (p_tx, p_th)[t % 2][:].rearrange("p (c t) -> p c t", c=DC)
                              ).then_inc(s_xnT, 1)

            def measure(t):
                for i in range(2):
                    if t < 4:
                        dve.wait_ge(s_x0[t + i], 16)
                    else:
                        dve.wait_ge(s_x[(t + i) % 4], 16 * (t // 4))
                    ins = v.bn_stats(stats[:, i, :], x_tile(t + i))
                link(ins)
                for i in range(2):
                    ins = v.bn_aggr(mv[:, t + i, :], stats[:, i, :])
                ins.then_inc(s_var, 1)

            def factors(t):
                ts = slice(t, t + 2)
                dve.wait_ge(s_std, t // 2 + 1)
                link(v.reciprocal(rstd[:, ts], std[:, ts]))
                v.scalar_tensor_tensor(out=nmr[:, ts], in0=mv[:, ts, 0], scalar=-1.0, in1=rstd[:, ts],
                                       op0=ALU.mult, op1=ALU.mult).then_inc(s_norm, 1)

            def decays():
                dve.wait_ge(s_dece, 1)
                v.tensor_scalar(dec[:, 2, :], dec[:, 1, :], 1.0, None, ALU.add).then_inc(s_dec, 1)
                dve.wait_ge(s_dec, 1)
                v.reciprocal(dec[:, 1, :], dec[:, 2, :]).then_inc(s_dec, 1)
                dve.wait_ge(s_dec, 2)
                v.tensor_scalar(dec[:, 3, :], dec[:, 1, :], -1.0, 1.0, ALU.mult, ALU.add
                                ).then_inc(s_dec, 1)

            def ie(ap):
                return ap.rearrange("p (i e) -> p i e", e=E)

            def ei(ap):
                return ap.rearrange("p (e i) -> p e i", i=TILES)

            def over_e(ap):
                return ap.unsqueeze(2).to_broadcast([P, TILES, E])

            def over_i(ap):
                return ap.unsqueeze(2).to_broadcast([P, E, TILES])

            def less_max():
                dve.wait_ge(s_lg, TILES)
                link(v.tensor_reduce(r16[:, 0, :], ie(p_a[:]), AX, ALU.max))
                v.tensor_tensor(ie(ra), ie(p_a[:]), over_e(r16[:, 0, :]), ALU.subtract
                                ).then_inc(s_lgm, 1)

            def softmax():
                dve.wait_ge(s_ex, 1)
                link(v.tensor_reduce(r16[:, 1, :], ie(rb), AX, ALU.add))
                link(v.reciprocal(r16[:, 2, :], r16[:, 1, :]))
                link(v.tensor_tensor(ie(ra), ie(rb), over_e(r16[:, 2, :]), ALU.mult))

            def top_values():
                for i in range(TILES):
                    ins = v.max(top8[:, i, :], ra[:, i * E:(i + 1) * E])
                link(ins)

            def top_index():
                for i in range(TILES):
                    ins = v.max_index(idx8[:, i, :], top8[:, i, :], ra[:, i * E:(i + 1) * E])
                link(ins)
                link(v.tensor_copy(idxf[:], idx8[:]))

            def choices():
                dve.wait_ge(s_const, 8)
                for k in range(TOPK):
                    ins = v.tensor_tensor(ei(eq[:, k, :]), over_i(iota_e[:]),
                                          idxf[:, :, k].unsqueeze(1).to_broadcast([P, E, TILES]),
                                          ALU.is_equal)
                ins.then_inc(s_eq, 1)

            def payload():
                link(v.tensor_reduce(r16[:, 3, :], top8[:, :, 0:TOPK], AX, ALU.add))
                link(v.tensor_scalar(r16[:, 4, :], r16[:, 3, :], 1e-20, None, ALU.add))
                link(v.reciprocal(r16[:, 5, :], r16[:, 4, :]))
                by_ki = pay[:].rearrange("p (k i) two -> p k i two", k=TOPK)
                v.tensor_copy(by_ki[:, :, :, 0], tok_id[:].unsqueeze(1).to_broadcast([P, TOPK, TILES]))
                link(v.tensor_tensor(by_ki[:, :, :, 1], top8[:, :, 0:TOPK].rearrange("p i k -> p k i"),
                                     r16[:, 5, :].unsqueeze(1).to_broadcast([P, TOPK, TILES]), ALU.mult))

            cap, nx, xend, xbase, s0, shift, shift2 = (r32[:, i, :] for i in range(7))

            def ranks():
                dve.wait_ge(s_cn, 1)
                dve.wait_ge(s_reset, 2)
                link(v.tensor_tensor_scan(rb, reset, p_b[:], 0.0, ALU.mult, ALU.add))
                link(v.tensor_tensor(ra, rb, p_b[:], ALU.subtract))
                link(v.tensor_tensor(rc, ra, p_a[:], ALU.add))

            def extra_slots():
                link(v.tensor_scalar(cap, ei(rb)[:, :, TILES - 1], float(CAP), -float(EPB * P),
                                     ALU.min, ALU.add))
                link(v.tensor_scalar(nx, cap, 0.0, float(P), ALU.is_gt, ALU.mult))
                for m in range(1, CAP // P - EPB):
                    link(v.tensor_scalar(xend, cap, float(m * P), float(P), ALU.is_gt, ALU.mult))
                    link(v.tensor_tensor(nx, nx, xend, ALU.add))
                link(v.tensor_tensor_scan(xend, ei(reset)[:, :, 1], nx, 0.0, ALU.mult, ALU.add))
                link(v.tensor_tensor(xbase, xend, nx, ALU.subtract))

            def slots():
                link(v.tensor_scalar(s0, xbase, float(MAINB * P - EPB * P), None, ALU.add))
                link(v.tensor_tensor(shift, s0, e384[:], ALU.subtract))
                link(v.tensor_tensor(shift2, trash[:], s0, ALU.subtract))
                link(v.tensor_tensor(ei(rb), ei(rc), over_i(e384[:]), ALU.add))

            def far_slots(least, by):
                link(v.tensor_scalar(ra, rc, float(least), None, ALU.is_ge))
                link(v.tensor_tensor(ei(ra), ei(ra), over_i(by), ALU.mult))
                link(v.tensor_tensor(rb, rb, ra, ALU.add))

            def extra_range():
                far_slots(EPB * P, shift)

            def nobody_reads():
                far_slots(CAP, shift2)

            def choice_slot(k):
                link(v.tensor_tensor(ra, eq[:, k, :], rb, ALU.mult))
                link(v.tensor_reduce(slot_f[:, k, :], ra.rearrange("p (e i) -> p i e", e=E), AX,
                                     ALU.add))
                if k == TOPK - 1:
                    v.tensor_copy(slot_i[:].rearrange("p c one -> p (c one)"),
                                  slot_f[:].rearrange("p k i -> p (k i)")).then_inc(s_slots, 1)

            def extra_experts(k0):
                w = TE // E
                link(v.tensor_tensor(ie(ra), xend.unsqueeze(1).to_broadcast([P, w, E]),
                                     blk128[:, k0:k0 + w].unsqueeze(2).to_broadcast([P, w, E]),
                                     ALU.is_le))
                link(v.tensor_reduce(eidf[:, k0:k0 + w], ie(ra), AX, ALU.add))

            def extra_blocks():
                link(v.tensor_scalar(eid[:], eidf[:], float(E - 1), None, ALU.min))
                link(v.tensor_scalar(cnt_i[:, 1:2], xend[:, E - 1:E], float(2 * P - 1), None, ALU.add))
                link(v.tensor_scalar(cnt_i[:, 2:3], cnt_i[:, 1:2], 8, None, ALU.logical_shift_right))
                v.tensor_scalar(cnt_i[:, 0:1], cnt_i[:, 2:3], -float(XMID // 2), 0.0, ALU.add, ALU.max
                                ).then_inc(s_route, 1)

            def h(b):
                dve.wait_ge(s_sg, b + 1)
                dve.wait_ge(s_ud, b + 1)
                v.tensor_tensor(h_sb[:], sg[:], p_u[:, 0:F], ALU.mult).then_inc(s_h, 1)

            def split_hT(b):
                dve.wait_ge(s_hth, b + 1)
                low(hT_lo[:, 0:FC - 1].rearrange("p c t -> p (c t)"), p_th[:, 0:(FC - 1) * P],
                    hT_hi[:, 0:FC - 1].rearrange("p c t -> p (c t)"))
                low(hT_lo[0:FLAST, FC - 1], p_th[0:FLAST, (FC - 1) * P:FC * P],
                    hT_hi[0:FLAST, FC - 1]).then_inc(s_ht, 1)

            def h_hT(b, between=None):
                h(b)
                if between is not None:
                    between()
                split_hT(b)

            def x_lo(t, par):
                dve.wait_ge(s_xth, t + 1)
                low(xT_lo[:, par], xnT[:, :, bass.ds(P * t, P)], xT_hi[:, par]).then_inc(s_xt, 1)

            FIRST_NTH = 2 * (TILES - 4) // 4

            def shared_out(t, slot, nth):
                dve.wait_ge(s_x[slot], 16 * (nth + 1))
                v.tensor_tensor(xring[:, slot, :], xring[:, slot, :], bias_b[:], ALU.add
                                ).then_inc(s_xbias, 1)
                dve.wait_ge(s_xbias, t + 1)
                dve.wait_ge(s_dd, 2 * t + 2)
                if isinstance(t, int) and t < 2:
                    dve.wait_ge(s_bst[t], 16 * BASES)
                else:
                    dve.wait_ge(s_sst[slot % 2], 8 * (t - slot % 2))
                v.tensor_tensor(y_sb[slot % 2], p_y[slot % 2][:], xring[:, slot, :], ALU.add
                                ).then_inc(s_ysh, 1)

            def w_lo_T(i, c):
                dve.wait_ge(s_wth, DC * i + c + 1)
                low((w_inT, w_outT)[i][1][:, c, :], p_y[c % 2][:], (w_inT, w_outT)[i][0][:, c, :]
                    ).then_inc(s_wT, 1)

            def xb_lo(b):
                dve.wait_ge(s_xbh, b + 1)
                low(xb[1], xnT[:, :, b * S:(b + 1) * S], xb[0]).then_inc(s_xb, 1)

            def scans(b, parts=()):
                for m in range(DC):
                    dve.wait_ge(s_q, DC * b + m + 1)
                    if b >= 1:
                        dve.wait_ge(s_st, DC * b)
                    v.tensor_tensor_scan(scan[:, m, :], dec[:, 1, m:m + 1].to_broadcast([P, S]),
                                         q_sb[:, m % 2], 0.0, ALU.mult, ALU.add).then_inc(s_sc, 1)
                    for part in parts[m:m + 1]:
                        part()

            def st_lo(b):
                for m in range(DC):
                    dve.wait_ge(s_sth, DC * b + m + 1)
                    low(st[1][:, m, :], scan[:, m, :], st[0][:, m, :]).then_inc(s_st, 1)

            def base(b, parts=()):
                for t in range(TPB * b, TPB * (b + 1)):
                    dve.wait_ge(s_out, t + 1)
                    if t < 4:
                        v.tensor_tensor(first[t], p_y[t % 2][:], first[t], ALU.add).then_inc(s_base, 1)
                    else:
                        dve.wait_ge(s_x[t % 4], 16 * (TILES // 4 - 1 + t // 4))
                        if t == 4:
                            for i in range(4):
                                dve.wait_ge(s_xns[i], 16 * TILES // 4)
                            dve.wait_ge(s_xnt, TILES)
                        if t >= 6:
                            dve.wait_ge(s_bst[t % 2], 16 * (t // 2 - 2))
                        v.tensor_tensor(y_sb[t % 2], p_y[t % 2][:], xring[:, t % 4, :], ALU.add
                                        ).then_inc(s_base, 1)
                    for part in parts[t % TPB:t % TPB + 1]:
                        part()

            dve.wait_ge(s_wgt, 1)
            v.tensor_copy(wgT[:].rearrange("p c e -> p (c e)"), p_b[:, 0:DC * E]).then_inc(s_wgT, 1)
            measure(0)
            factors(0)
            measure(2)
            factors(2)
            for t in range(4):
                tile_evac(t)
            w_lo_T(0, 0)
            w_lo_T(0, 1)
            xb_lo(0)
            w_lo_T(0, 2)
            w_lo_T(0, 3)
            measure(4)
            factors(4)
            measure(6)
            factors(6)
            decays()

            def between(b):
                def after_first():
                    w_lo_T(1, 2 * b)
                    w_lo_T(1, 2 * b + 1)
                    measure(4 * b + 8)

                def after_second():
                    factors(4 * b + 8)
                    tile_evac(4 * b + 4)
                    tile_evac(4 * b + 5)
                    measure(4 * b + 10)

                def after_third():
                    factors(4 * b + 10)
                    tile_evac(4 * b + 6)
                    tile_evac(4 * b + 7)

                return after_first, after_second, after_third

            dve.wait_ge(s_zero, 32)
            scans(0, between(0))
            xb_lo(1)
            st_lo(0)
            scans(1, between(1))
            for t in range(12, TILES):
                tile_evac(t)
            xb_lo(2)
            less_max()
            base(0, [softmax, top_values, top_index])
            st_lo(1)
            scans(2, [choices, payload])
            xb_lo(3)
            base(1)
            st_lo(2)
            scans(3, [ranks, extra_slots, lambda: extra_experts(0), lambda: extra_experts(TILES)])
            base(2, [lambda: w_lo_piece(0, 0, 0), lambda: w_lo_piece(0, 1, 1), lambda: x_lo(0, 0)])
            st_lo(3)
            w_lo_piece(0, 2, 2)
            base(3, [lambda: h(0), lambda: split_hT(0), lambda: x_lo(1, 1)])
            for j in range(3):
                w_lo_piece(1, j, 3 + j)
            dve.wait_ge(s_biasl, 16)

            def xt_lo(i, par):
                dve.wait_ge(s_xth, i + TILES + 1)
                low(xT_lo[:, par].rearrange("p c t -> p (c t)"), p_tx[:],
                    xT_hi[:, par].rearrange("p c t -> p (c t)")).then_inc(s_xt, 1)

            def shared_pair(it, j, parts=(None, None, None, None)):
                t = 4 * it + j
                h_hT(2 * t, parts[0])
                x_lo(t + 1, 1 - j % 2)
                shared_out(t - 1, (j - 1) % 4, it + (FIRST_NTH if j else FIRST_NTH - 1))
                if parts[1] is not None:
                    parts[1]()
                h_hT(2 * t + 1, parts[2])
                if parts[3] is not None:
                    parts[3]()

            h_hT(1, lambda: extra_experts(2 * TILES))
            extra_experts(3 * TILES)
            choice = [lambda k=k: choice_slot(k) for k in range(TOPK)]
            shared_pair(0, 1, (extra_blocks, None, slots, extra_range))
            shared_pair(0, 2, (nobody_reads, None, choice[0], choice[1]))
            shared_pair(0, 3, (choice[2], choice[3], choice[4], choice[5]))
            with dve.Fori(1, TILES // 4 - 1) as it:
                for j in range(4):
                    shared_pair(it, j)
            for j in range(3):
                shared_pair(TILES // 4 - 1, j)
            dve.wait_ge(s_tabt, 1)
            n = MAINB
            for dst, lo, hi in ((ids[:, 0:n], 0, n), (wts[:, 0:n], n, 2 * n),
                                (ids[:, n:COLS], 2 * n, 2 * n + XMAX),
                                (wts[:, n:COLS], 2 * n + XMAX, 2 * n + 2 * XMAX)):
                v.tensor_copy(dst, p_b[:, lo:hi]).then_inc(s_tab, 1)
            h_hT(SHARED - 2)
            xt_lo(0, 0)
            w_lo_piece(0, 0, 6)
            shared_out(TILES - 2, 2, FIRST_NTH + 3)
            h_hT(SHARED - 1, lambda: w_lo_piece(0, 1, 7))

            def round_(it, last):
                def split(m, j):
                    return m % 2, j, 18 * it + 3 * m + j + 6

                for j in range(STEPS):
                    i = STEPS * it + j
                    middle = j in MIDDLE and not (last and MIDDLE[j][0] == 6)
                    h_hT(i + SHARED, (lambda: w_lo_piece(*split(*MIDDLE[j]))) if middle else None)
                    if isinstance(it, int) and i == 0:
                        shared_out(TILES - 1, 3, FIRST_NTH + 3)
                    if not last or j + 2 < STEPS:
                        xt_lo(i + 2, j % 2)
                    if not last or SPLITS[j][0] < 6:
                        w_lo_piece(*split(*SPLITS[j]))

            xt_lo(1, 1)
            w_lo_piece(0, 2, 8)
            round_(0, False)
            with dve.Fori(1, ROUNDS - 1) as it:
                round_(it, False)
            round_(ROUNDS - 1, True)
            dve.wait_ge(s_route, 1)
            more = dve.value_load(cnt_i[0:1, 0:1], min_val=0, max_val=(XMAX - XMID) // 2)
            with dve.If(more > 0):
                with dve.Fori(0, more) as k:
                    i = 2 * k + MIDB
                    for par in range(2):
                        for j in range(3):
                            w_lo_piece(par, j, 6 * k + 18 * ROUNDS + 6 + 3 * par + j)
                    for j in range(2):
                        xt_lo(i + j, j)
                    for j in range(2):
                        h_hT(i + j + SHARED)


_INS = ("x", "W_in", "W_out", "decay", "bias")
_NAMES = ["L0_attn_" + n for n in _INS] + ["L0_ffn_" + n for n in
                                           ("wg_router", "w_gate", "w_up", "w_down", "ws_gate",
                                            "ws_up", "ws_down")]


def kernel(**inputs):
    import numpy as np
    import concourse.bacc as bacc
    from concourse.bass_utils import run_bass_kernel_spmd

    nc = bacc.Bacc("TRN2", target_bir_lowering=False, num_devices=1)
    arrays, args = {}, []
    for name in _NAMES:
        a = np.ascontiguousarray(inputs[name])
        if name == "L0_attn_x":
            a = a.reshape(T, D)
        arrays[name] = a
        args.append(nc.dram_tensor(name, a.shape, mybir.dt.from_np(a.dtype), kind="ExternalInput").ap())
    out = nc.dram_tensor("out", (ROWS, D), F32, kind="ExternalOutput").ap()
    xn_rows = nc.dram_tensor("xn_rows", (ROWS, D), F32, kind="Internal").ap()
    table = nc.dram_tensor("slot_table", (TABLE + T * E, 2), F32, kind="Internal").ap()
    build(nc, *args, out, xn_rows, table)
    r = run_bass_kernel_spmd(nc, [arrays], core_ids=[0])
    return r.results[0]["out"][0:T].reshape(B, S, D)
```
